# Optimizing a Trainium2 kernel written in Bass

```python
import numpy as np
import jax
import jax.numpy as jnp

def _softmax(x, axis=-1):
    return jax.nn.softmax(x, axis=axis)

def _gelu(x):
    return jax.nn.gelu(x, approximate=True)

def _silu(x):
    return jax.nn.silu(x)

def _sigmoid(x):
    return jax.nn.sigmoid(x)

def _layernorm(x, axis=-1, eps=1e-05):
    m = jnp.mean(x, axis=axis, keepdims=True)
    v = jnp.var(x, axis=axis, keepdims=True)
    return (x - m) / jnp.sqrt(v + eps)

def _scatter_add(tgt, idx, src, axis=0):
    return tgt.at[idx].add(src)

def _segment_sum(src, seg, n):
    return jax.ops.segment_sum(src, seg, n)
kernel_name = 'mk_gnn_preln_d4_gnn_r64_ed8ad7'

def setup_inputs(seed: int=0):
    np.random.seed(seed)
    _w = jnp.asarray

    def _rec_inputs():
        import jax
        import jax.numpy as jnp
        _gk = jax.random.key(seed)
        x = -0.0001884 + 1 * jax.random.normal(jax.random.fold_in(_gk, 1), (50000, 256), jnp.float32)
        src = jax.random.randint(jax.random.fold_in(_gk, 2), (12500,), 0, 50000, jnp.int32)
        dst = jax.random.randint(jax.random.fold_in(_gk, 3), (12500,), 0, 50000, jnp.int32)
        _o = jnp.argsort(dst, stable=True)
        src = src[_o]
        dst = dst[_o]
        edge_weight = -0.000423496 + 0.100023 * jax.random.normal(jax.random.fold_in(_gk, 13), (12500,), jnp.float32)
        return (x, src, dst, edge_weight)
    x, src, dst, edge_weight = _rec_inputs()

    def _L0_gnn_setup():
        import jax, jax.numpy as jnp
        import numpy as np
        BLOCK_DIMS = [8] * 32

        def _mask_indices():
            d = sum(BLOCK_DIMS)
            mask = np.ones((d, d), dtype=np.int8)
            off = 0
            for b in BLOCK_DIMS:
                mask[off:off + b, off:off + b] = 0
                off += b
            rows, cols = np.nonzero(mask)
            return (d, rows.astype(np.int32), cols.astype(np.int32))
        key = jax.random.key(seed)
        k1, k2 = jax.random.split(key)
        d, rows, cols = _mask_indices()
        N = 500000
        X = jax.random.normal(k1, (N, d), dtype=jnp.float32)
        w_est = 0.1 * jax.random.normal(k2, (rows.shape[0],), dtype=jnp.float32)
        return {'X': X, 'w_est': w_est, 'rows': jnp.asarray(rows), 'cols': jnp.asarray(cols)}
    _L0_gnn_all = _L0_gnn_setup()
    _L0_gnn_in = {k: v for k, v in _L0_gnn_all.items() if k in ()}
    del _L0_gnn_all

    def _L1_gnn_setup():
        import jax, jax.numpy as jnp
        import numpy as np
        N_NODES = 100000
        N_EDGES = 25000
        D = 256
        key = jax.random.key(seed)
        ks = jax.random.split(key, 8)
        h6_all = jax.random.normal(ks[0], (N_NODES, D), dtype=jnp.float32)
        edge_index = jax.random.randint(ks[1], (2, N_EDGES), 0, N_NODES, dtype=jnp.int64)
        edge_weight = jax.random.uniform(ks[2], (N_EDGES,), dtype=jnp.float32)
        s = 1.0 / np.sqrt(D)
        W = jax.random.normal(ks[3], (D, D), dtype=jnp.float32) * s
        b = jnp.zeros((D,), dtype=jnp.float32)
        W1 = jax.random.normal(ks[4], (D, D), dtype=jnp.float32) * s
        b1 = jnp.zeros((D,), dtype=jnp.float32)
        W2 = jax.random.normal(ks[5], (D, D), dtype=jnp.float32) * s
        b2 = jnp.zeros((D,), dtype=jnp.float32)
        return {'h6_all': h6_all, 'edge_index': edge_index, 'edge_weight': edge_weight, 'W': W, 'b': b, 'W1': W1, 'b1': b1, 'W2': W2, 'b2': b2}
    _L1_gnn_all = _L1_gnn_setup()
    _L1_gnn_in = {k: v for k, v in _L1_gnn_all.items() if k in ('W', 'b', 'W1', 'b1', 'W2', 'b2')}
    del _L1_gnn_all

    def _L2_gnn_setup():
        import jax, jax.numpy as jnp
        import numpy as np
        N_NODES = 100000
        N_EDGES = 50000
        D_FEAT = 256
        LEAKY_ALPHA = 0.2
        key = jax.random.key(seed)
        k1, k2, k3 = jax.random.split(key, 3)
        x = jax.random.normal(k1, (N_NODES, D_FEAT), dtype=jnp.float32)
        edge_index = jax.random.randint(k2, (2, N_EDGES), 0, N_NODES, dtype=jnp.int32)
        W = jax.random.normal(k3, (D_FEAT, D_FEAT), dtype=jnp.float32) * (1.0 / np.sqrt(D_FEAT))
        b = jnp.zeros((D_FEAT,), dtype=jnp.float32)
        return {'x': x, 'edge_index': edge_index, 'W': W, 'b': b}
    _L2_gnn_all = _L2_gnn_setup()
    _L2_gnn_in = {k: v for k, v in _L2_gnn_all.items() if k in ('W', 'b')}
    del _L2_gnn_all

    def _L3_gnn_setup():
        import jax, jax.numpy as jnp
        import numpy as np
        N = 50000
        E = 25000
        D = 256
        H = 256
        EPS = 1e-05

        def _gnn_layer(x, row, col, W, b, g, beta):
            n = x.shape[0]
            neigh = x[col]
            agg = jax.ops.segment_sum(neigh, row, num_segments=n)
            deg = jax.ops.segment_sum(jnp.ones((row.shape[0],), x.dtype), row, num_segments=n)
            deg = jnp.maximum(deg, 1.0)[:, None]
            h = (x + agg / deg) @ W.T + b
            mu = jnp.mean(h, axis=-1, keepdims=True)
            var = jnp.mean(jnp.square(h - mu), axis=-1, keepdims=True)
            hn = (h - mu) * jax.lax.rsqrt(var + EPS) * g + beta
            return jax.nn.silu(hn)
        key = jax.random.key(seed)
        ks = jax.random.split(key, 12)
        x = jax.random.normal(ks[0], (N, D), dtype=jnp.float32)
        edge_index = jax.random.randint(ks[1], (2, E), 0, N, dtype=jnp.int32)
        s0 = 1.0 / np.sqrt(D)
        s1 = 1.0 / np.sqrt(H)
        W0 = jax.random.uniform(ks[2], (H, D), jnp.float32, -s0, s0)
        b0 = jax.random.uniform(ks[3], (H,), jnp.float32, -s0, s0)
        g0 = jnp.ones((H,), jnp.float32)
        beta0 = jnp.zeros((H,), jnp.float32)
        W1 = jax.random.uniform(ks[4], (H, H), jnp.float32, -s1, s1)
        b1 = jax.random.uniform(ks[5], (H,), jnp.float32, -s1, s1)
        g1 = jnp.ones((H,), jnp.float32)
        beta1 = jnp.zeros((H,), jnp.float32)
        return {'x': x, 'edge_index': edge_index, 'W0': W0, 'b0': b0, 'g0': g0, 'beta0': beta0, 'W1': W1, 'b1': b1, 'g1': g1, 'beta1': beta1}
    _L3_gnn_all = _L3_gnn_setup()
    _L3_gnn_in = {k: v for k, v in _L3_gnn_all.items() if k in ('W0', 'b0', 'g0', 'beta0', 'W1', 'b1', 'g1', 'beta1')}
    del _L3_gnn_all
    return {'x': x, 'src': src, 'dst': dst, 'edge_weight': edge_weight, 'L1_gnn_W': _L1_gnn_in['W'], 'L1_gnn_b': _L1_gnn_in['b'], 'L1_gnn_W1': _L1_gnn_in['W1'], 'L1_gnn_b1': _L1_gnn_in['b1'], 'L1_gnn_W2': _L1_gnn_in['W2'], 'L1_gnn_b2': _L1_gnn_in['b2'], 'L2_gnn_W': _L2_gnn_in['W'], 'L2_gnn_b': _L2_gnn_in['b'], 'L3_gnn_W0': _L3_gnn_in['W0'], 'L3_gnn_b0': _L3_gnn_in['b0'], 'L3_gnn_g0': _L3_gnn_in['g0'], 'L3_gnn_beta0': _L3_gnn_in['beta0'], 'L3_gnn_W1': _L3_gnn_in['W1'], 'L3_gnn_b1': _L3_gnn_in['b1'], 'L3_gnn_g1': _L3_gnn_in['g1'], 'L3_gnn_beta1': _L3_gnn_in['beta1']}

def reference(x, src, dst, edge_weight, L1_gnn_W, L1_gnn_b, L1_gnn_W1, L1_gnn_b1, L1_gnn_W2, L1_gnn_b2, L2_gnn_W, L2_gnn_b, L3_gnn_W0, L3_gnn_b0, L3_gnn_g0, L3_gnn_beta0, L3_gnn_W1, L3_gnn_b1, L3_gnn_g1, L3_gnn_beta1):
    import jax
    import jax.numpy as jnp

    def _L0_gnn_ref(X, w_est, rows, cols):
        import jax, jax.numpy as jnp
        import numpy as np
        BLOCK_DIMS = [8] * 32

        def _mask_indices():
            d = sum(BLOCK_DIMS)
            mask = np.ones((d, d), dtype=np.int8)
            off = 0
            for b in BLOCK_DIMS:
                mask[off:off + b, off:off + b] = 0
                off += b
            rows, cols = np.nonzero(mask)
            return (d, rows.astype(np.int32), cols.astype(np.int32))
        d = X.shape[1]
        W = jnp.zeros((d, d), dtype=X.dtype).at[rows, cols].set(w_est)
        return X @ W

    def _L1_gnn_ref(h6_all, edge_index, edge_weight, W, b, W1, b1, W2, b2):
        import jax, jax.numpy as jnp
        import numpy as np
        N_NODES = 100000
        N_EDGES = 25000
        D = 256
        'GCNConv(256->256, weighted, self-loops, symmetric norm) + 2-layer MLP head.'
        N = h6_all.shape[0]
        row, col = (edge_index[0], edge_index[1])
        sl = jnp.arange(N, dtype=edge_index.dtype)
        row_sl = jnp.concatenate([row, sl])
        col_sl = jnp.concatenate([col, sl])
        ew_sl = jnp.concatenate([edge_weight, jnp.ones((N,), dtype=edge_weight.dtype)])
        deg = jax.ops.segment_sum(ew_sl, row_sl, num_segments=N)
        dinv = jnp.where(deg > 0, jax.lax.rsqrt(deg), 0.0)
        norm = dinv[row_sl] * ew_sl * dinv[col_sl]
        xw = h6_all @ W
        msgs = xw[col_sl] * norm[:, None]
        h7 = jax.ops.segment_sum(msgs, row_sl, num_segments=N) + b
        h = jax.nn.relu(h7 @ W1 + b1)
        out = h @ W2 + b2
        return out

    def _L2_gnn_ref(x, edge_index, W, b):
        import jax, jax.numpy as jnp
        import numpy as np
        N_NODES = 100000
        N_EDGES = 50000
        D_FEAT = 256
        LEAKY_ALPHA = 0.2
        N = x.shape[0]
        row = edge_index[0]
        col = edge_index[1]
        ones = jnp.ones(row.shape[0], dtype=x.dtype)
        deg = jax.ops.segment_sum(ones, row, num_segments=N)
        deg_safe = jnp.where(deg > 0, deg, 1.0)
        dinv_sqrt = jnp.where(deg > 0, jax.lax.rsqrt(deg_safe), 0.0)
        w = dinv_sqrt[row] * dinv_sqrt[col]
        h = jax.ops.segment_sum(w[:, None] * x[col], row, num_segments=N)
        h = h @ W + b
        return jnp.where(h >= 0, h, LEAKY_ALPHA * h)

    def _L3_gnn_ref(x, edge_index, W0, b0, g0, beta0, W1, b1, g1, beta1):
        import jax, jax.numpy as jnp
        import numpy as np
        N = 50000
        E = 25000
        D = 256
        H = 256
        EPS = 1e-05

        def _gnn_layer(x, row, col, W, b, g, beta):
            n = x.shape[0]
            neigh = x[col]
            agg = jax.ops.segment_sum(neigh, row, num_segments=n)
            deg = jax.ops.segment_sum(jnp.ones((row.shape[0],), x.dtype), row, num_segments=n)
            deg = jnp.maximum(deg, 1.0)[:, None]
            h = (x + agg / deg) @ W.T + b
            mu = jnp.mean(h, axis=-1, keepdims=True)
            var = jnp.mean(jnp.square(h - mu), axis=-1, keepdims=True)
            hn = (h - mu) * jax.lax.rsqrt(var + EPS) * g + beta
            return jax.nn.silu(hn)
        row, col = (edge_index[0], edge_index[1])
        x = _gnn_layer(x, row, col, W0, b0, g0, beta0)
        x = _gnn_layer(x, row, col, W1, b1, g1, beta1)
        return x
    edge_index = jnp.stack([src, dst])
    h = jnp.maximum(_layernorm(x, axis=-1), 0.0)
    x = x + _L0_gnn_ref(h, edge_weight, src, dst)
    h = jnp.maximum(_layernorm(x, axis=-1), 0.0)
    x = x + _L1_gnn_ref(h, edge_index, edge_weight, L1_gnn_W, L1_gnn_b, L1_gnn_W1, L1_gnn_b1, L1_gnn_W2, L1_gnn_b2)
    h = jnp.maximum(_layernorm(x, axis=-1), 0.0)
    x = x + _L2_gnn_ref(h, edge_index, L2_gnn_W, L2_gnn_b)
    h = jnp.maximum(_layernorm(x, axis=-1), 0.0)
    x = x + _L3_gnn_ref(h, edge_index, L3_gnn_W0, L3_gnn_b0, L3_gnn_g0, L3_gnn_beta0, L3_gnn_W1, L3_gnn_b1, L3_gnn_g1, L3_gnn_beta1)
    return x

_drawn_inputs = setup_inputs


def setup_inputs(seed=0):
    import zlib

    import numpy as np

    out = dict(_drawn_inputs(seed))
    spreads = {'L1_gnn_b': (0.0, 0.1),
     'L1_gnn_b1': (0.0, 0.1),
     'L1_gnn_b2': (0.0, 0.1),
     'L2_gnn_b': (0.0, 0.1),
     'L3_gnn_g0': (1.0, 0.2),
     'L3_gnn_beta0': (0.0, 0.1),
     'L3_gnn_g1': (1.0, 0.2),
     'L3_gnn_beta1': (0.0, 0.1)}
    factors = {}
    for name, (base, spread) in spreads.items():
        noise = np.random.default_rng([zlib.crc32(name.encode()), seed]).standard_normal(out[name].shape)
        drawn = base * np.exp(spread * noise) if base else spread * noise
        out[name] = jnp.asarray(drawn.astype(out[name].dtype))
    for name, factor in factors.items():
        out[name] = (out[name] * factor).astype(out[name].dtype)
    return out
```

```python
from contextlib import ExitStack

import numpy as np

import concourse.bass as bass
from concourse import mybir

P = 128
D = 256
NODES = 50000
EDGES = 12500
LO = 256
HI = 256
TILES = -(-EDGES // P)
EG = 14
EGROUPS = TILES // EG
NG = 12
NROWS = NG * P
NGROUPS = -(-NODES // NROWS)
LAST = NODES - NROWS
EP, NPAIR = EG // 2, NG // 2
BG = 7
BGROUPS = TILES // BG
NONE = TILES * P
PAD_NODE = HI * LO - 1
NF = 8
N_START, N_LAST, N_DINV, N_DINV2, N_WINV, N_MEAN, N_LASTF = range(7)
RF = 8
R_SRC, R_DST, R_LAST, R_C1, R_C2, R_C3, R_SELF = range(7)
EPS = 1e-5
ALPHA = 0.2

F32 = mybir.dt.float32
BF16 = mybir.dt.bfloat16
I32 = mybir.dt.int32
U32 = mybir.dt.uint32
ALU = mybir.AluOpType
ACT = mybir.ActivationFunctionType

PHASES = [("edges1", EGROUPS), ("edges2", EGROUPS), ("edges3", EGROUPS), ("edges4", EGROUPS),
          ("nodes", NGROUPS)]


class Signal:

    def __init__(self, sem, before, per, step=1):
        self.sem, self.per, self.base, self.step = sem, dict(zip([p for p, _ in PHASES], per)), {}, step
        n = before
        for name, passes in PHASES:
            self.base[name] = n
            n += self.per[name] * passes
        self.total = n

    def at(self, phase, i, k):
        return (i * self.per[phase] + (self.base[phase] + k + 1)) * self.step

    def all(self, phase):
        passes = dict(PHASES)[phase]
        return (self.base[phase] + self.per[phase] * passes) * self.step


def gnn_stack(nc, ins, out, scratch):
    x = ins["x"]
    node_tab, rec_sorted, rec_groups = scratch["node_tab"], scratch["rec_sorted"], scratch["rec_groups"]
    state, table = scratch["state"], scratch["table"]
    column = [scratch[f"column{k}"] for k in range(3)]

    with ExitStack() as ctx:
        def sb(name, shape, dt=F32):
            return ctx.enter_context(nc.sbuf_tensor(name, shape, dt))

        def sem(name):
            return ctx.enter_context(nc.semaphore(name))

        bank = [ctx.enter_context(nc.psum_tensor(f"bank{j}", [P, 512], F32)) for j in range(8)]
        banks = bank
        sum_bank, spread_bank = bank[5:7], bank[7]

        def turn_ring(ph):
            return bank[0:3] if ph == "nodes" else bank[0:2]

        def prod_ring(ph):
            return bank[3:8] if ph == "nodes" else bank[2:5]

        ident = sb("ident", [P, P])
        earlier = sb("earlier", [P, P])
        later = sb("later", [P, P])
        ones = sb("ones", [P, P])
        ones_b = sb("ones_b", [P, P], BF16)
        zeros_b = sb("zeros_b", [P, 512], BF16)
        count_f = sb("count_f", [P, LO])
        count_b = sb("count_b", [P, LO], BF16)
        part = sb("part", [P, 2])
        is_last = sb("is_last", [P, 1])
        minus_half = sb("minus_half", [P, EG])
        eps_w = sb("eps_w", [P, EG])
        W_mask = sb("W_mask", [P, 2, D])
        W_gcn = sb("W_gcn", [P, 2, D])
        W_head = sb("W_head", [P, 2, D])
        W_sum = sb("W_sum", [P, 2, D])
        W_av0 = sb("W_av0", [P, 2, D])
        W_av1 = sb("W_av1", [P, 2, D])
        b_cols = sb("b_cols", [P, 2, 4])
        b_gcn = sb("b_gcn", [P, 2])
        b_rows = sb("b_rows", [P, 3, D], BF16)
        b_sum = sb("b_sum", [P, D])
        g_last = sb("g_last", [P, 2, D])
        beta_last = sb("beta_last", [P, 2, D])
        none_row = sb("none_row", [1, 4 * D])

        rec_land = sb("rec_land", [P, EG * RF])
        rec_now = sb("rec_now", [P, EG, RF])
        node_land = sb("node_land", [P, NG * NF])
        node_now = sb("node_now", [P, NG, NF])
        src_before = sb("src_before", [P, 1])
        rows = sb("rows", [P, EG, D])
        resid = sb("resid", [P, EG, D])
        resid3 = sb("resid3", [P, NG, D])
        left = sb("left", [P, EG, D])
        turned = sb("turned", [P, EG, D])
        hidden = sb("hidden", [P, 2, EG, P])
        skip = sb("skip", [P, NG, D])

        home = [b_[:, :, :].rearrange("p t f -> p (t f)") for b_ in (resid, left, turned, resid3, skip)]
        room = [EG * D, EG * D, EG * D, NG * D, NG * D]
        taken = [0] * 5

        def early(name, shape, dt=F32):
            size = int(np.prod(shape[1:]))
            words = size // 2 if dt == BF16 else size
            words += words % 2
            k = next(k for k in range(5) if taken[k] + words <= room[k])
            flat = home[k][0:shape[0], taken[k]:taken[k] + words]
            taken[k] += words
            if dt != F32:
                flat = flat.bitcast(dt)
            flat = flat[:, 0:size]
            if len(shape) == 2:
                return flat
            dims = "abcd"[:len(shape) - 1]
            return flat.rearrange(f"p ({' '.join(dims)}) -> p {' '.join(dims)}",
                                  **{d: n for d, n in zip(dims, shape[1:])})

        b_part = early("b_part", [P, 3, 3, D], BF16)
        b_rest = early("b_rest", [P, 3, D])
        b_three = early("b_three", [P, 3, D])
        w_turn = early("w_turn", [P, 2, D])
        edge_in = early("edge_in", [TILES, 3, P], I32)
        ew_in = early("ew_in", [TILES, P])
        edge_lohi = early("edge_lohi", [TILES, 2, P], I32)
        edge_f = early("edge_f", [TILES, 4, P])
        cols = early("cols", [P, 5, TILES])
        C_SRC, C_DST, C_LO, C_HI, C_EW = range(5)
        cols_i = early("cols_i", [P, 2, TILES], I32)
        key = early("key", [P, TILES])
        to_spread = early("to_spread", [P, TILES, 3])
        spread_now = early("spread_now", [P, 2, 3])
        dst_cut = early("dst_cut", [P, TILES])
        first_hi = early("first_hi", [P, TILES])
        ew_part = early("ew_part", [P, 3, TILES])
        ew_b = early("ew_b", [P, 3, TILES], BF16)
        ew_rest = early("ew_rest", [P, 2, TILES])
        in_tile = early("in_tile", [P, TILES])
        in_before = early("in_before", [P, TILES])
        place = early("place", [P, TILES])
        oh_lo = early("oh_lo", [P, 2, LO], BF16)
        oh_hi = early("oh_hi", [P, 2, HI], BF16)
        oh_lo_w = early("oh_lo_w", [P, 2, 3, LO], BF16)
        oh_dst = early("oh_dst", [P, 2, LO], BF16)
        oh_dst_w = early("oh_dst_w", [P, 2, 3, LO], BF16)
        oh_turn = early("oh_turn", [P, 2, 2, P])
        junk = early("junk", [P, 2, 2, LO], BF16)
        again = early("again", [P, 2])
        keep = early("keep", [P, 2])
        hits = early("hits", [P, 512])
        counts = early("counts", [P, 2, LO])
        scan = early("scan", [P, 2, LO])
        ones_w = early("ones_w", [P, LO])
        half_w = early("half_w", [P, 2, LO])
        base = early("base", [P, 2])
        idx2 = [early(f"idx2_{h}", [P, 2, BG], I32) for h in range(2)]
        ns = [early(f"ns_{h}", [P, BG, NF]) for h in range(2)]
        nd = [early(f"nd_{h}", [P, BG, NF]) for h in range(2)]
        rec = [early(f"rec_{h}", [P, BG, RF]) for h in range(2)]
        rec_at = [early(f"rec_at_{h}", [P, BG], I32) for h in range(2)]
        rec_all = early("rec_all", [P, TILES, RF])


        pre = sb("pre", [P, EG, D])
        got = sb("got", [P, NG, 4 * D])
        got_flat = got[:, :, :].rearrange("p t f -> p (t f)")

        def at_got(start, n, shape, **sizes):
            return got_flat[:, start:start + n].rearrange(shape, **sizes)

        got_e = at_got(0, EG * D, "p (t f) -> p t f", f=D)
        sums = at_got(EG * D, EG * D, "p (t f) -> p t f", f=D)
        same = at_got(2 * EG * D, EG * P, "p (t f) -> p t f", f=P)
        goes_on = at_got(2 * EG * D + EG * P, EG * P, "p (t f) -> p t f", f=P)
        node_rec = at_got(0, 2 * LO * NF, "p (c l f) -> p c l f", c=2, l=LO)
        w_in = hidden[:, :, :, :].rearrange("p c t r -> p (c t r)")[:, 0:8 * D].rearrange(
            "p (w c n) -> p w c n", w=4, c=2)
        tmp = pre[:, :, :].rearrange("p t f -> p (t f)")[:, 0:8 * LO].rearrange(
            "p (n c l) -> p n c l", n=4, c=2)
        stats = sb("stats", [P, EG, 6])
        moments = sb("moments", [P, EG, 2])
        var_eps = sb("var_eps", [P, EG])
        rstd = sb("rstd", [P, EG])
        stats_l = sb("stats_l", [P, NG, 6])
        moments_l = sb("moments_l", [P, NG, 2])
        var_eps_l = sb("var_eps_l", [P, NG])
        rstd_l = sb("rstd_l", [P, NG])

        N_LOADS = 34
        DVE_ZEROS, DVE_EDGE_F, DVE_W_TURN, DVE_NONE_ROW, DVE_READY = 1, 5, 7, 25, 25
        DVE_SCAN, DVE_ROOT1, DVE_ROOT2, DVE_NODE_REC = 27, 29, 43, 48

        dve_past, pool_past = sem("dve_past"), sem("pool_past")
        s_ld = sem("inputs_loaded")
        s_ms = sem("pads_set")
        s_cst = sem("constants_set")
        s_pool = sem("pool_setup_step")
        s_dve = sem("dve_setup_step")
        s_pe = sem("pe_setup_step")
        s_roots = sem("roots_ready")
        cols_picked = sem("cols_picked")
        spread_done = sem("spread_done")
        turn_hot_ready = sem("turn_hot_ready")
        hot_ready = sem("hot_ready")
        dup_counted = sem("dup_counted")
        keep_ready = sem("keep_ready")
        oh_dst_ready = sem("oh_dst_ready")
        look_done = sem("look_done")
        hist_done = sem("hist_done")
        hist_copied = sem("hist_copied")
        pairs_done = sem("pairs_done")
        weights_done = sem("weights_done")
        hits_copied = sem("hits_copied")
        mask_updated = sem("mask_updated")
        node_stored = sem("node_records_stored")
        idx_ready = [sem("idx_ready_even"), sem("idx_ready_odd")]
        ends_gathered = [sem("ends_gathered_even"), sem("ends_gathered_odd")]
        rec_step = [sem("rec_step_even"), sem("rec_step_odd")]
        rec_ready = [sem("rec_ready_even"), sem("rec_ready_odd")]
        rec_scattered = [sem("rec_scattered_even"), sem("rec_scattered_odd")]
        rec_loaded_all = sem("rec_loaded_all")
        rec_grouped = sem("rec_grouped")

        E, N = EP, NPAIR
        PRIME = 32
        S = lambda name, per, before=PRIME, step=1: Signal(sem(name), before, per, step)
        rec_loaded = S("rec_loaded", [1, 1, 1, 1, 1], 0, 16)
        work_ready = S("work_ready", [1, 1, 1, 1, 1])
        rows_loaded = S("rows_loaded", [0, 1, 1, 1, 1], 0, 16)
        gathered = S("gathered", [EG, EG, EG, EG, NG], 0, 16)
        stats_done = S("stats_done", [2 * E, 2 * E, E, 2 * E, 4 * N])
        moments_ready = S("moments_ready", [2 * E, 2 * E, E, 2 * E, 4 * N])
        eps_added = S("eps_added", [2 * E, 2 * E, E, 2 * E, 4 * N])
        rstd_raw = S("rstd_raw", [0, E, 0, 0, N])
        rstd_ready = S("rstd_ready", [2 * E, 2 * E, E, 2 * E, 4 * N])
        normed = S("normed", [2 * E, 2 * E, E, 2 * E, 4 * N])
        plus_ready = S("plus_ready", [0, E, 0, E, 2 * N])
        turn_done = S("turn_done", [E, 2 * E, 0, 2 * E, 4 * N])
        turned_ready = S("turned_ready", [E, 2 * E, 0, 2 * E, 4 * N])
        hidden_done = S("hidden_done", [0, E, 0, 0, N])
        hidden_ready = S("hidden_ready", [0, E, 0, 0, N])
        product = S("product", [E, 2 * E, 0, 2 * E, 4 * N])
        resid_ready = S("resid_ready", [E, E, E, 0, 2 * N])
        resid_stored = S("resid_stored", [1, 1, 1, 0, 0], 1, 16)
        src_spread = S("src_spread", [E, E, E, E, 0])
        same_ready = S("same_ready", [E, E, E, E, 0])
        src_kept = S("src_kept", [1, 1, 1, 1, 0])
        message_ready = S("message_ready", [E, E, E, E, 0])
        summed = S("summed", [EG, EG, EG, EG, 0])
        sums_copied = S("sums_copied", [EG, EG, EG, EG, 0])
        biased = S("biased", [0, E, 0, 0, 0])
        leaky_ready = S("leaky_ready", [0, E, 0, 0, 0])
        table_stored = S("table_stored", [2, 2, 2, 1, 0], 4, 16)
        skip_ready = S("skip_ready", [0, 0, 0, 0, N])
        pre_ready = S("pre_ready", [0, 0, 0, 0, N])
        stats_done_l = S("stats_done_l", [0, 0, 0, 0, N])
        moments_ready_l = S("moments_ready_l", [0, 0, 0, 0, N])
        eps_added_l = S("eps_added_l", [0, 0, 0, 0, N])
        rstd_ready_l = S("rstd_ready_l", [0, 0, 0, 0, N])
        normed_l = S("normed_l", [0, 0, 0, 0, N])
        gained = S("gained", [0, 0, 0, 0, N])
        shifted = S("shifted", [0, 0, 0, 0, N])
        silu_ready = S("silu_ready", [0, 0, 0, 0, N])
        out_ready = S("out_ready", [0, 0, 0, 0, N])
        out_stored = S("out_stored", [0, 0, 0, 0, 1], 1, 16)
        primed = [work_ready, stats_done, moments_ready, eps_added, rstd_raw, rstd_ready, normed, plus_ready,
                  turn_done, turned_ready, hidden_done, hidden_ready, product, resid_ready,
                  src_spread, same_ready, src_kept, message_ready, summed, sums_copied, biased, leaky_ready,
                  skip_ready, pre_ready, stats_done_l, moments_ready_l, eps_added_l, rstd_ready_l, normed_l,
                  gained, shifted, silu_ready, out_ready]

        MEASURED = {"edges1": 2, "edges2": 2, "edges3": 1, "edges4": 2, "nodes": 4}
        TURNED = {"edges1": 1, "edges2": 2, "edges3": 0, "edges4": 2, "nodes": 4}
        HIDDEN = {"edges2": 0, "nodes": 1}

        SLOTS = 4 * NPAIR

        def pair_at(n, k):
            return (n - k) // 2 if n >= k and (n - k) % 2 == 0 and (n - k) // 2 < NPAIR else None

        def pairs(ph):
            return NPAIR if ph == "nodes" else EP

        def rows_to_turn(ph, i, n):
            stage, j = divmod(n, pairs(ph))
            plus = {"edges2": [0], "edges4": [0], "nodes": [1, 2]}.get(ph, [])
            if stage in plus:
                return plus_ready.sem, plus_ready.at(ph, i, plus.index(stage) * pairs(ph) + j)
            return normed.sem, normed.at(ph, i, n)

        def product_read(ph, i, k, back):
            stage, j = divmod(k, pairs(ph))
            by = {("edges1", 0): (resid_ready, j), ("edges2", 0): (resid_ready, j),
                  ("edges2", 1): (message_ready, j), ("edges4", 0): (normed, EP + j),
                  ("edges4", 1): (message_ready, j), ("nodes", 0): (resid_ready, j),
                  ("nodes", 1): (resid_ready, NPAIR + j), ("nodes", 2): (normed, 3 * NPAIR + j),
                  ("nodes", 3): (pre_ready, j)}
            signal, index = by[ph, stage]
            return signal.sem, signal.at(ph, i, index - back * signal.per[ph])

        block = ctx.enter_context(nc.Block())

        @block.sync
        def _(sp):
            full = (TILES - 1) * P
            sp.wait_ge(s_ms, 4)
            for n, name in enumerate(["src", "dst"]):
                sp.dma_start(edge_in[0:TILES - 1, n, :],
                             ins[name][0:full].rearrange("(t p) -> t p", p=P)).then_inc(s_ld, 16)
                sp.dma_start(edge_in[TILES - 1:TILES, n, 0:EDGES - full],
                             ins[name][full:EDGES].rearrange("(a p) -> a p", a=1)).then_inc(s_ld, 16)
            sp.dma_start(ew_in[0:TILES - 1, :],
                         ins["edge_weight"][0:full].rearrange("(t p) -> t p", p=P)).then_inc(s_ld, 16)
            sp.dma_start(ew_in[TILES - 1:TILES, 0:EDGES - full],
                         ins["edge_weight"][full:EDGES].rearrange("(a p) -> a p", a=1)).then_inc(s_ld, 16)
            for n, name in enumerate(["L1_gnn_W", "L1_gnn_W1", "L3_gnn_W0", "L3_gnn_W1"]):
                sp.dma_start(w_in[:, n, :, :],
                             ins[name].rearrange("(c p) n -> p c n", p=P)).then_inc(s_ld, 16)
            for name, to in (("L1_gnn_W2", W_head), ("L2_gnn_W", W_sum)):
                sp.dma_start(to[:, :, :], ins[name].rearrange("(c p) n -> p c n", p=P)).then_inc(s_ld, 16)
            for n, name in enumerate(["L1_gnn_b", "L1_gnn_b1", "L3_gnn_g0", "L3_gnn_beta0"]):
                for c in range(2):
                    sp.dma_start(b_cols[:, c, n:n + 1], ins[name][c * P:(c + 1) * P]
                                 .rearrange("(p a) -> p a", a=1)).then_inc(s_ld, 16)
            for n, name in enumerate(["L1_gnn_b2", "L3_gnn_b0", "L3_gnn_b1"]):
                for k in range(3):
                    sp.dma_start(b_three[32 * k:32 * k + 1, n, :],
                                 ins[name].rearrange("(a n) -> a n", a=1)).then_inc(s_ld, 16)
            for name, to in (("L2_gnn_b", b_sum[:, :]), ("L3_gnn_g1", g_last[:, 0, :]), ("L3_gnn_g1", g_last[:, 1, :]),
                             ("L3_gnn_beta1", beta_last[:, 0, :]), ("L3_gnn_beta1", beta_last[:, 1, :])):
                sp.dma_start(to, ins[name].rearrange("(a n) -> a n", a=1)
                             .to_broadcast([P, D])).then_inc(s_ld, 16)

            sp.wait_ge(s_dve, DVE_NONE_ROW)
            sp.dma_start(table[NONE:NONE + 1, :], none_row[:, :]).then_inc(table_stored.sem, 16)
            for k in range(3):
                sp.dma_start(column[k][NONE:NONE + 1, :],
                             none_row[:, k * D:(k + 1) * D]).then_inc(table_stored.sem, 16)
            for n, s in enumerate((resid_stored, out_stored)):
                sp.dma_start(scratch["begin"][n:n + 1, :], none_row[:, 0:D]).then_inc(s.sem, 16)
            sp.wait_ge(s_dve, DVE_NODE_REC)
            sp.dma_start(node_tab.rearrange("(c p l) f -> p c (l f)", c=2, p=P),
                         node_rec[:, :, :, :].rearrange("p c l f -> p c (l f)")).then_inc(node_stored, 16)

            for h in range(2):
                sp.wait_ge(rec_scattered[h], 16 * (TILES // 2))
            sp.dma_start(rec_all[:, :, :], rec_sorted.rearrange("(t p) f -> p t f", p=P)).then_inc(rec_loaded_all, 16)
            sp.wait_ge(rec_loaded_all, 16)
            sp.dma_start(rec_groups.rearrange("i p f -> p i f"),
                         rec_all[:, :, :].rearrange("p (i t) f -> p i (t f)", i=EGROUPS)).then_inc(rec_grouped, 16)
            sp.wait_ge(rec_grouped, 16)

            def load_rec(ph, i):
                sp.dma_start(rec_land[:, :], rec_groups[bass.ds(i, 1), :, :]
                             .rearrange("a p f -> (a p) f")).then_inc(rec_loaded.sem, 16)

            def load_state(ph, i):
                sp.dma_start(rows[:, 0:EG, :], state[bass.ds(i, 1), :, :, :]
                             .rearrange("a p t f -> (a p) t f")).then_inc(rows_loaded.sem, 16)

            def store_edges(ph, i):
                k = int(ph[-1]) - 1
                if ph != "edges4":
                    sp.wait_ge(resid_ready.sem, resid_ready.at(ph, i, EP - 1))
                    sp.dma_start(state[bass.ds(i, 1), :, :, :].rearrange("a p t f -> (a p) t f"),
                                 resid[:, 0:EG, :]).then_inc(resid_stored.sem, 16)
                if ph == "edges2":
                    sp.wait_ge(leaky_ready.sem, leaky_ready.at(ph, i, EP - 1))
                else:
                    sp.wait_ge(sums_copied.sem, sums_copied.at(ph, i, EG - 1))
                what = pre if ph == "edges2" else sums
                sp.dma_start(table[bass.ds(i * (EG * P), EG * P), k * D:(k + 1) * D]
                             .rearrange("(t p) f -> p t f", p=P), what[:, 0:EG, :]).then_inc(table_stored.sem, 16)
                if k < 3:
                    sp.dma_start(column[k][bass.ds(i * (EG * P), EG * P), :]
                                 .rearrange("(t p) f -> p t f", p=P), what[:, 0:EG, :]).then_inc(table_stored.sem, 16)

            def load_next(ph, i):
                sp.wait_ge(work_ready.sem, work_ready.at(ph, i, 0))
                sp.wait_ge(gathered.sem, gathered.at(ph, i, EG - 1))
                load_rec(ph, i + 1)
                if ph != "edges1":
                    if ph == "edges4":
                        sp.wait_ge(normed.sem, normed.at(ph, i, EP - 1))
                    else:
                        sp.wait_ge(resid_ready.sem, resid_ready.at(ph, i, EP - 1))
                    load_state(ph, i + 1)

            for n, (ph, passes) in enumerate(PHASES[:-1]):
                if n:
                    before = PHASES[n - 1][0]
                    sp.wait_ge(gathered.sem, gathered.all(before))
                    sp.wait_ge(work_ready.sem, work_ready.all(before))
                load_rec(ph, 0)
                if n:
                    sp.wait_ge(resid_stored.sem, resid_stored.all(before))
                    load_state(ph, 0)
                with sp.Fori(0, passes - 1) as i:
                    load_next(ph, i)
                    store_edges(ph, i)
                store_edges(ph, passes - 1)

            ph = "nodes"

            def load_nodes(row):
                sp.dma_start(node_land[:, :], node_tab[bass.ds(row, NROWS), :]
                             .rearrange("(p t) f -> p (t f)", p=P)).then_inc(rec_loaded.sem, 16)

            def load_rows(row):
                sp.dma_start(rows[:, 0:NG, :], x[bass.ds(row, NROWS), :]
                             .rearrange("(p t) f -> p t f", p=P)).then_inc(rows_loaded.sem, 16)

            def next_nodes(i, row):
                sp.wait_ge(work_ready.sem, work_ready.at(ph, i, 0))
                sp.wait_ge(gathered.sem, gathered.at(ph, i, NG - 1))
                load_nodes(row)
                sp.wait_ge(resid_ready.sem, resid_ready.at(ph, i, NPAIR - 1))
                load_rows(row)

            def store_nodes(i, row):
                sp.wait_ge(out_ready.sem, out_ready.at(ph, i, NPAIR - 1))
                sp.dma_start(out[bass.ds(row, NROWS), :].rearrange("(p t) f -> p t f", p=P),
                             pre[:, 0:NG, :]).then_inc(out_stored.sem, 16)

            sp.wait_ge(normed.sem, normed.all("edges4"))
            sp.wait_ge(gathered.sem, gathered.all("edges4"))
            sp.wait_ge(work_ready.sem, work_ready.all("edges4"))
            load_nodes(0)
            load_rows(0)
            next_nodes(0, NROWS)
            with sp.Fori(1, NGROUPS - 2) as i:
                next_nodes(i, i * NROWS + NROWS)
                store_nodes(i - 1, i * NROWS - NROWS)
            next_nodes(NGROUPS - 2, LAST)
            store_nodes(NGROUPS - 3, (NGROUPS - 3) * NROWS)
            store_nodes(NGROUPS - 2, (NGROUPS - 2) * NROWS)
            sp.wait_ge(out_stored.sem, out_stored.at(ph, NGROUPS - 2, 0))
            store_nodes(NGROUPS - 1, LAST)
            sp.wait_ge(out_stored.sem, out_stored.all(ph))
            sp.wait_ge(table_stored.sem, table_stored.all("edges4"))
            sp.wait_ge(resid_stored.sem, resid_stored.all("edges3"))

        @block.gpsimd
        def _(pool):
            for s in primed:
                pool.sem_inc(s.sem, PRIME)
            nc.gpsimd.memset(ident[:, :], 0.0).then_inc(s_pool, 1)
            nc.gpsimd.memset(earlier[:, :], 1.0).then_inc(s_pool, 1)
            nc.gpsimd.memset(later[:, :], 1.0).then_inc(s_pool, 1)
            nc.gpsimd.memset(is_last[:, :], 0.0).then_inc(s_pool, 1)
            pool.wait_ge(s_pool, 4)
            nc.gpsimd.affine_select(out=ident[:, :], in_=ident[:, :], compare_op=ALU.not_equal, fill=1.0,
                                    base=0, pattern=[[-1, P]], channel_multiplier=1).then_inc(s_cst, 1)
            nc.gpsimd.affine_select(out=earlier[:, :], in_=earlier[:, :], compare_op=ALU.is_gt, fill=0.0,
                                    base=0, pattern=[[-1, P]], channel_multiplier=1).then_inc(s_cst, 1)
            nc.gpsimd.affine_select(out=later[:, :], in_=later[:, :], compare_op=ALU.is_gt, fill=0.0,
                                    base=0, pattern=[[1, P]], channel_multiplier=-1).then_inc(s_cst, 1)
            nc.gpsimd.affine_select(out=is_last[:, :], in_=is_last[:, :], compare_op=ALU.not_equal, fill=1.0,
                                    base=-(P - 1), pattern=[[0, 1]], channel_multiplier=1).then_inc(s_cst, 1)
            nc.gpsimd.iota(count_f[:, :], [[1, LO]], base=0, channel_multiplier=0,
                           allow_small_or_imprecise_dtypes=True).then_inc(s_cst, 1)
            nc.gpsimd.iota(part[:, :], [[P, 2]], base=0, channel_multiplier=1,
                           allow_small_or_imprecise_dtypes=True).then_inc(s_cst, 1)

            def gather_ends(i, h):
                pool.wait_ge(idx_ready[h], i * 2 + 2)
                pool.sem_inc(pool_past, 1)
                for g in range(BG):
                    for n, to in ((0, ns[h]), (1, nd[h])):
                        nc.gpsimd.indirect_dma_start(
                            to[:, g, :], None, node_tab,
                            bass.IndirectOffsetOnAxis(ap=idx2[h][:, n, g:g + 1], axis=0),
                            bounds_check=HI * LO - 1).then_inc(ends_gathered[h], 16)

            def scatter_records(i, h):
                pool.wait_ge(rec_ready[h], i + 1)
                pool.sem_inc(pool_past, 1)
                for g in range(BG):
                    nc.gpsimd.indirect_dma_start(
                        rec_sorted, bass.IndirectOffsetOnAxis(ap=rec_at[h][:, g:g + 1], axis=0),
                        rec[h][:, g, :], None, bounds_check=TILES * P - 1).then_inc(rec_scattered[h], 16)

            pool.wait_ge(node_stored, 16)
            gather_ends(0, 0)
            with pool.Fori(0, BGROUPS // 2 - 1) as i:
                gather_ends(i, 1)
                scatter_records(i, 0)
                gather_ends(i + 1, 0)
                scatter_records(i, 1)
            gather_ends(BGROUPS // 2 - 1, 1)
            scatter_records(BGROUPS // 2 - 1, 0)
            scatter_records(BGROUPS // 2 - 1, 1)

            def power(ph, i, n, own=None):
                a = 2 * (n % pairs(ph))
                b = a + 2
                pool.wait_ge(moments_ready.sem, moments_ready.at(ph, i, n))
                nc.gpsimd.tensor_tensor(var_eps[:, a:b], moments[:, a:b, 1], eps_w[:, a:b],
                                        ALU.add).then_inc(eps_added.sem, 1)
                pool.wait_ge(eps_added.sem, eps_added.at(ph, i, n))
                if own is None:
                    nc.gpsimd.tensor_tensor(rstd[:, a:b], var_eps[:, a:b], minus_half[:, a:b],
                                            ALU.pow).then_inc(rstd_ready.sem, 1)
                else:
                    nc.gpsimd.tensor_tensor(rstd[:, a:b], var_eps[:, a:b], minus_half[:, a:b],
                                            ALU.pow).then_inc(rstd_raw.sem, 1)
                    pool.wait_ge(rstd_raw.sem, rstd_raw.at(ph, i, n % pairs(ph)))
                    nc.gpsimd.tensor_tensor(rstd[:, a:b], rstd[:, a:b], own[:, a:b],
                                            ALU.mult).then_inc(rstd_ready.sem, 1)

            def gather_edges(ph, src, field, j):
                pool.sem_inc(pool_past, 1)
                for g in (2 * j, 2 * j + 1):
                    nc.gpsimd.indirect_dma_start(
                        rows[:, g, :] if ph == "edges1" else got_e[:, g, :], None, src,
                        bass.IndirectOffsetOnAxis(
                            ap=rec_land[:, g * RF + field:g * RF + field + 1].bitcast(I32), axis=0),
                        bounds_check=src.shape[0] - 1).then_inc(gathered.sem, 16)

            def edges_pass(ph, src, field, i, last):
                for n in range(MEASURED[ph] * EP):
                    if ph == "edges2" and n < EP:
                        if n == 0:
                            pool.wait_ge(work_ready.sem, work_ready.at(ph, i, 0))
                        power(ph, i, n, rec_now[:, :, R_SELF])
                    else:
                        power(ph, i, n)
                if not last:
                    pool.wait_ge(rec_loaded.sem, rec_loaded.at(ph, i + 1, 0))
                    for j in range(EP):
                        if ph in ("edges1", "edges3"):
                            pool.wait_ge(resid_ready.sem, resid_ready.at(ph, i, j))
                        else:
                            pool.wait_ge(plus_ready.sem, plus_ready.at(ph, i, j))
                        gather_edges(ph, src, field, j)

            for ph, field, src in (("edges1", R_DST, x), ("edges2", R_LAST, column[0]),
                                   ("edges3", R_LAST, column[1]), ("edges4", R_LAST, column[2])):
                if ph != "edges1":
                    before = f"edges{int(ph[-1]) - 1}"
                    pool.wait_ge(table_stored.sem, table_stored.all(before))
                    pool.wait_ge(plus_ready.sem, plus_ready.all(before))
                    pool.wait_ge(resid_ready.sem, resid_ready.all(before))
                pool.wait_ge(rec_loaded.sem, rec_loaded.at(ph, 0, 0))
                for j in range(EP):
                    gather_edges(ph, src, field, j)
                with pool.Fori(0, EGROUPS - 1) as i:
                    edges_pass(ph, src, field, i, False)
                edges_pass(ph, src, field, EGROUPS - 1, True)

            ph = "nodes"

            def gather_nodes(j):
                pool.sem_inc(pool_past, 1)
                for g in (2 * j, 2 * j + 1):
                    nc.gpsimd.indirect_dma_start(
                        got[:, g, :], None, table,
                        bass.IndirectOffsetOnAxis(
                            ap=node_land[:, g * NF + N_LAST:g * NF + N_LAST + 1].bitcast(I32), axis=0),
                        bounds_check=NONE).then_inc(gathered.sem, 16)

            def nodes_slot(i, n, main, before):
                s, j = divmod(n, NPAIR)
                if main:
                    if s == 1:
                        if j == 0:
                            pool.wait_ge(work_ready.sem, work_ready.at(ph, i, 0))
                        power(ph, i, n, node_now[:, :, N_DINV2])
                    else:
                        power(ph, i, n)
                m = pair_at(n, 1)
                if before and m is not None:
                    a, b = 2 * m, 2 * m + 2
                    pool.wait_ge(moments_ready_l.sem, moments_ready_l.at(ph, i, m - NPAIR))
                    nc.gpsimd.tensor_tensor(var_eps_l[:, a:b], moments_l[:, a:b, 1], eps_w[:, a:b],
                                            ALU.add).then_inc(eps_added_l.sem, 1)
                    pool.wait_ge(eps_added_l.sem, eps_added_l.at(ph, i, m - NPAIR))
                    nc.gpsimd.tensor_tensor(rstd_l[:, a:b], var_eps_l[:, a:b], minus_half[:, a:b],
                                            ALU.pow).then_inc(rstd_ready_l.sem, 1)
                if main and s == 0:
                    if before:
                        pool.wait_ge(pre_ready.sem, pre_ready.at(ph, i, j - NPAIR))
                    if j == 0:
                        pool.wait_ge(rec_loaded.sem, rec_loaded.at(ph, i, 0))
                    gather_nodes(j)
                m = pair_at(n, 3)
                if before and m is not None:
                    a, b = 2 * m, 2 * m + 2
                    pool.wait_ge(normed_l.sem, normed_l.at(ph, i, m - NPAIR))
                    nc.gpsimd.tensor_tensor(pre[:, a:b, :], pre[:, a:b, :], g_last[:, :, :],
                                            ALU.mult).then_inc(gained.sem, 1)
                    pool.wait_ge(gained.sem, gained.at(ph, i, m - NPAIR))
                    nc.gpsimd.tensor_tensor(pre[:, a:b, :], pre[:, a:b, :], beta_last[:, :, :],
                                            ALU.add).then_inc(shifted.sem, 1)
                if main and s == 1:
                    if j == 0:
                        pool.wait_ge(gathered.sem, gathered.at(ph, i, NG - 1))
                    pool.wait_ge(resid_ready.sem, resid_ready.at(ph, i, j))
                    nc.gpsimd.tensor_tensor(skip[:, 2 * j:2 * j + 2, :], resid[:, 2 * j:2 * j + 2, :],
                                            got[:, 2 * j:2 * j + 2, D:2 * D],
                                            ALU.add).then_inc(skip_ready.sem, 1)

            pool.wait_ge(table_stored.sem, table_stored.all("edges4"))
            pool.wait_ge(plus_ready.sem, plus_ready.all("edges4"))
            for n in range(SLOTS):
                nodes_slot(0, n, True, False)
            with pool.Fori(1, NGROUPS) as i:
                for n in range(SLOTS):
                    nodes_slot(i, n, True, True)
            for n in range(SLOTS):
                nodes_slot(NGROUPS, n, False, True)

        @block.scalar
        def _(act):
            act.wait_ge(s_dve, DVE_READY)

            def pick(t, q):
                nc.scalar.copy(spread_now[:, q, :], to_spread[:, bass.ds(t, 1), :].rearrange("p a n -> p (a n)")
                               ).then_inc(cols_picked, 1)

            def one_edge_tile(t, q, more):
                if more:
                    act.wait_ge(spread_done, t + 1)
                    pick(t + 2, q)
                act.wait_ge(oh_dst_ready, t + 1)
                for k in range(3):
                    done = nc.scalar.activation(oh_dst_w[:, q, k, :], oh_dst[:, q, :], ACT.Copy,
                                                scale=ew_part[:, k, bass.ds(t, 1)])
                done.then_inc(hot_ready, 1)
                act.wait_ge(pairs_done, t + 1)
                act.wait_ge(mask_updated, t + 2)
                nc.scalar.copy(hits[:, :], banks[5][:, :]).then_inc(hits_copied, 1)
                act.wait_ge(hist_done, t + 1)
                nc.scalar.copy(counts[:, :, :].rearrange("p c l -> p (c l)"), banks[6][:, :]).then_inc(hist_copied, 1)

            pick(0, 0)
            pick(1, 1)
            with act.Fori(0, TILES // 2 - 1) as i:
                for q in range(2):
                    one_edge_tile(i * 2 + q, q, True)
            one_edge_tile(TILES - 2, 0, False)
            one_edge_tile(TILES - 1, 1, False)
            act.wait_ge(s_dve, DVE_ROOT1)
            nc.scalar.activation(tmp[:, 2, :, :], tmp[:, 0, :, :], ACT.Sqrt).then_inc(s_roots, 1)
            act.wait_ge(s_dve, DVE_ROOT2)
            nc.scalar.activation(tmp[:, 0, :, :], tmp[:, 3, :, :], ACT.Sqrt).then_inc(s_roots, 1)

            def evacuate(ph, i, n, func):
                a = 2 * (n % pairs(ph))
                ring = turn_ring(ph)
                act.wait_ge(turn_done.sem, turn_done.at(ph, i, n))
                nc.scalar.activation(turned[:, a:a + 2, :], ring[n % len(ring)][:, :]
                                     .rearrange("p (t f) -> p t f", f=D), func).then_inc(turned_ready.sem, 1)

            def evacuate_silu(ph, i, n):
                a = 2 * (n % pairs(ph))
                ring = turn_ring(ph)
                act.wait_ge(turn_done.sem, turn_done.at(ph, i, n))
                for c in range(2):
                    done = nc.scalar.activation(
                        turned[:, a:a + 2, c * P:(c + 1) * P],
                        ring[n % len(ring)][:, :].rearrange("p (t f) -> p t f", f=D)[:, :, c * P:(c + 1) * P],
                        ACT.Silu, bias=b_cols[:, c, 3:4], scale=b_cols[:, c, 2:3])
                done.then_inc(turned_ready.sem, 1)

            def hide(ph, i, n):
                j = n % pairs(ph)
                ring = prod_ring(ph)
                act.wait_ge(hidden_done.sem, hidden_done.at(ph, i, j))
                for c in range(2):
                    done = nc.scalar.activation(
                        hidden[:, c, 2 * j:2 * j + 2, :], ring[n % len(ring)][:, c * D:c * D + D]
                        .rearrange("p (t r) -> p t r", r=P), ACT.Relu, bias=b_gcn[:, c:c + 1])
                done.then_inc(hidden_ready.sem, 1)

            def copy_sums(ph, i):
                if ph == "edges2":
                    act.wait_ge(leaky_ready.sem, leaky_ready.at(ph, i, -1))
                act.wait_ge(table_stored.sem, table_stored.at(ph, i, -1))
                for g in range(EG):
                    act.wait_ge(summed.sem, summed.at(ph, i, g))
                    nc.scalar.copy(sums[:, g, :], sum_bank[g % 2][:, 0:D]).then_inc(sums_copied.sem, 1)

            def act_slot(ph, i, n):
                stage = n // pairs(ph)
                if n < TURNED[ph] * pairs(ph):
                    if (ph, stage) in (("edges1", 0), ("edges2", 1), ("nodes", 0)):
                        evacuate(ph, i, n, ACT.Relu)
                    elif (ph, stage) in (("edges4", 1), ("nodes", 3)):
                        evacuate_silu(ph, i, n)
                    else:
                        evacuate(ph, i, n, ACT.Copy)
                if n >= 1 and HIDDEN.get(ph) == (n - 1) // pairs(ph):
                    hide(ph, i, n - 1)

            def nodes_slot(i, n, main, before):
                m = pair_at(n, 3)
                if before and m is not None:
                    act.wait_ge(shifted.sem, shifted.at("nodes", i, m - NPAIR))
                    nc.scalar.activation(pre[:, 2 * m:2 * m + 2, :], pre[:, 2 * m:2 * m + 2, :],
                                         ACT.Silu).then_inc(silu_ready.sem, 1)
                if main:
                    act_slot("nodes", i, n)

            for ph, passes in PHASES[:-1]:
                with act.Fori(0, passes) as i:
                    for n in range(TURNED[ph] * EP + 1):
                        act_slot(ph, i, n)
                    copy_sums(ph, i)
            for n in range(SLOTS):
                nodes_slot(0, n, True, False)
            with act.Fori(1, NGROUPS) as i:
                for n in range(SLOTS):
                    nodes_slot(i, n, True, True)
            for n in range(SLOTS):
                nodes_slot(NGROUPS, n, False, True)

        @block.tensor
        def _(pe):
            def turn(to, what, n=P, start=True):
                return nc.tensor.transpose(to, what, ident[0:n, 0:n])

            pe.wait_ge(s_cst, 6)
            pe.wait_ge(s_dve, DVE_EDGE_F)
            for n in range(4):
                turn(banks[0][:, n * TILES:(n + 1) * TILES], edge_f[:, n, :], TILES)
            turn(banks[0][:, 4 * TILES:5 * TILES], ew_in[:, :], TILES).then_inc(s_pe, 1)
            for n, b in ((0, 1), (2, 2), (3, 3)):
                for c in range(2):
                    for r in range(2):
                        last = turn(banks[b][:, c * D + r * P:c * D + (r + 1) * P],
                                    w_in[:, n, r, c * P:(c + 1) * P])
            last.then_inc(s_pe, 1)
            pe.wait_ge(s_dve, DVE_W_TURN)
            for c in range(2):
                for k in range(2):
                    pe.matmul(banks[4][:, c * D:(c + 1) * D], w_turn[:, k, c * P:(c + 1) * P],
                              w_in[:, 1, k, :], start=(k == 0), stop=(k == 1))
            for c in range(2):
                for k in range(2):
                    last = pe.matmul(banks[5][:, c:c + 1], w_in[:, 1, k, c * P:(c + 1) * P],
                                     b_cols[:, k, 0:1], start=(k == 0), stop=(k == 1))
            last.then_inc(s_pe, 1)
            pe.wait_ge(s_dve, DVE_ZEROS)
            pe.matmul(banks[6][:, :], zeros_b[:, 0:P], zeros_b[:, :], start=True, stop=True)
            pe.matmul(banks[7][:, :], zeros_b[:, 0:P], zeros_b[:, :], start=True, stop=True).then_inc(s_pe, 1)
            pe.wait_ge(s_dve, DVE_READY)

            def spread(t, q):
                pe.wait_ge(turn_hot_ready, t + 1)
                pe.wait_ge(cols_picked, t + 1)
                for n in range(3):
                    last = turn(banks[q][:, n * P:(n + 1) * P], spread_now[:, q, n:n + 1].to_broadcast([P, P]))
                last.then_inc(spread_done, 1)

            def one_edge_tile(t, q, more):
                pe.wait_ge(turn_hot_ready, t + 3)
                pe.wait_ge(hist_copied, t + 1)
                for c in range(2):
                    last = pe.matmul(banks[2 + q][:, 0:LO], oh_turn[:, q, c, :], counts[:, c, :],
                                     start=(c == 0), stop=(c == 1))
                last.then_inc(look_done, 1)
                pe.wait_ge(oh_dst_ready, t + 1)
                pe.wait_ge(mask_updated, t + 2)
                for c in range(2):
                    last = pe.matmul(banks[5][:, c * D:(c + 1) * D], oh_lo[:, q, c * P:(c + 1) * P],
                                     oh_dst[:, q, :], start=True, stop=True)
                last.then_inc(pairs_done, 1)
                for c in range(2):
                    pe.matmul(banks[6][:, c * LO:(c + 1) * LO], oh_hi[:, q, c * P:(c + 1) * P],
                              oh_lo[:, q, :], start=False, stop=True, skip_group_check=True)
                    for k in range(3):
                        last = pe.matmul(banks[7][:, c * LO:(c + 1) * LO], oh_hi[:, q, c * P:(c + 1) * P],
                                         oh_lo_w[:, q, k, :], start=False, stop=True, skip_group_check=True)
                last.then_inc(hist_done, 1)
                if more:
                    spread(t + 2, q)
                pe.wait_ge(hot_ready, t + 1)
                for c in range(2):
                    for k in range(3):
                        last = pe.matmul(banks[4][:, c * D:(c + 1) * D], oh_lo[:, q, c * P:(c + 1) * P],
                                         oh_dst_w[:, q, k, :], start=(k == 0), stop=(k == 2))
                last.then_inc(weights_done, 1)

            spread(0, 0)
            spread(1, 1)
            with pe.Fori(0, TILES // 2 - 1) as i:
                for q in range(2):
                    one_edge_tile(i * 2 + q, q, True)
            one_edge_tile(TILES - 2, 0, False)
            one_edge_tile(TILES - 1, 1, False)
            pe.wait_ge(s_dve, DVE_SCAN)
            pe.matmul(banks[0][:, 0:2], later[:, :], scan[:, :, LO - 1], start=True, stop=True)
            pe.matmul(banks[1][:, 0:1], ones[:, :], scan[:, 0, LO - 1:LO], start=True, stop=True).then_inc(s_pe, 1)

            def turn_pair(ph, i, n):
                ring = turn_ring(ph)
                pe.wait_ge(*rows_to_turn(ph, i, n))
                pe.wait_ge(turned_ready.sem, turned_ready.at(ph, i, n - len(ring) if n >= len(ring) else -1))
                for t in range(2):
                    for c in range(2):
                        o = t * D + c * P
                        last = turn(ring[n % len(ring)][:, o:o + P],
                                    left[:, 2 * (n % pairs(ph)) + t, c * P:(c + 1) * P])
                last.then_inc(turn_done.sem, 1)

            def spread_sources(ph, i, j):
                if j == 0:
                    pe.wait_ge(work_ready.sem, work_ready.at(ph, i, 0))
                pe.wait_ge(same_ready.sem, same_ready.at(ph, i, j - 1))
                for t in range(2):
                    last = turn(spread_bank[:, t * P:t * P + P],
                                rec_now[:, 2 * j + t, R_SRC:R_SRC + 1].to_broadcast([P, P]))
                last.then_inc(src_spread.sem, 1)

            def bank_free(ph, i, n):
                ring, steps = len(prod_ring(ph)), TURNED[ph] * pairs(ph)
                k = n % steps
                back = 1 if n < 0 else 0
                if k >= ring:
                    k -= ring
                else:
                    back += 1
                    k = max(m for m in range(steps) if m % ring == k)
                pe.wait_ge(*product_read(ph, i, k, back))

            def multiply(ph, i, n, weight, bias=None):
                k = n % (TURNED[ph] * pairs(ph))
                ring = prod_ring(ph)
                bank_ = ring[k % len(ring)]
                pe.wait_ge(turned_ready.sem, turned_ready.at(ph, i, n))
                bank_free(ph, i, n)
                for t in range(2):
                    o = bank_[:, t * D:t * D + D]
                    for c in range(2):
                        last = pe.matmul(o, turned[:, 2 * (k % pairs(ph)) + t, c * P:(c + 1) * P],
                                         weight[:, c, :], start=(c == 0), stop=(c == 1 and bias is None))
                    if bias is not None:
                        last = pe.matmul(o, ones_b[:, :], b_rows[:, bias, :], start=False, stop=True)
                last.then_inc(product.sem, 1)

            def multiply_hidden(ph, i, n):
                a = 2 * (n % pairs(ph))
                ring = prod_ring(ph)
                pe.wait_ge(turned_ready.sem, turned_ready.at(ph, i, n))
                bank_free(ph, i, n)
                for m in range(2):
                    for c in range(2):
                        last = pe.matmul(ring[n % len(ring)][:, m * D:m * D + D]
                                         .rearrange("p (t r) -> p t r", r=P),
                                         W_gcn[:, c, m * P:(m + 1) * P],
                                         turned[:, a:a + 2, c * P:(c + 1) * P],
                                         start=(c == 0), stop=(c == 1))
                last.then_inc(hidden_done.sem, 1)

            def multiply_head(ph, i, n):
                j = n % pairs(ph)
                ring = prod_ring(ph)
                pe.wait_ge(hidden_ready.sem, hidden_ready.at(ph, i, j))
                for t in range(2):
                    o = ring[n % len(ring)][:, t * D:t * D + D]
                    for c in range(2):
                        pe.matmul(o, hidden[:, c, 2 * j + t, :], W_head[:, c, :], start=(c == 0), stop=False)
                    last = pe.matmul(o, ones_b[:, :], b_rows[:, 0, :], start=False, stop=True)
                last.then_inc(product.sem, 1)

            def add_up(ph, i):
                def within(g):
                    pe.wait_ge(message_ready.sem, message_ready.at(ph, i, g // 2))
                    pe.wait_ge(sums_copied.sem, sums_copied.at(ph, i, g - 2 if g >= 2 else -1))
                    pe.matmul(sum_bank[g % 2][:, 0:D], same[:, g, :], left[:, g, :], start=True, stop=False)

                within(0)
                for g in range(EG):
                    if g + 1 < EG:
                        within(g + 1)
                    pe.wait_ge(sums_copied.sem, sums_copied.at(ph, i, g - 1))
                    pe.matmul(sum_bank[g % 2][:, 0:D], goes_on[:, g, :], sums[:, (g - 1) % EG, :],
                              start=False, stop=True).then_inc(summed.sem, 1)

            WEIGHTS = {"edges1": [(W_mask, None)], "edges2": [None, (W_sum, None)], "edges3": [],
                       "edges4": [(W_av0, 1), (W_av1, None)],
                       "nodes": [(W_mask, None), None, (W_av0, 1), (W_av1, 2)]}
            def product_of(ph, i, n):
                weight = WEIGHTS[ph][(n // pairs(ph)) % len(WEIGHTS[ph])]
                if weight is None:
                    multiply_hidden(ph, i, n)
                else:
                    multiply(ph, i, n, *weight)

            def pe_slot(ph, i, n, before):
                if ph != "nodes" and n < EP:
                    spread_sources(ph, i, n)
                if n < TURNED[ph] * pairs(ph):
                    turn_pair(ph, i, n)
                if n >= 2 and HIDDEN.get(ph) == (n - 2) // pairs(ph):
                    multiply_head(ph, i, n - 2)
                if 1 <= n <= TURNED[ph] * pairs(ph) or before:
                    product_of(ph, i, n - 1)

            for ph, passes in PHASES[:-1]:
                with pe.Fori(0, passes) as i:
                    for n in range(max(TURNED[ph] * EP + 1, EP)):
                        pe_slot(ph, i, n, False)
                    pe.wait_ge(same_ready.sem, same_ready.at(ph, i, EP - 1))
                    add_up(ph, i)
            pe.wait_ge(sums_copied.sem, sums_copied.all("edges4"))
            for n in range(SLOTS):
                pe_slot("nodes", 0, n, False)
            with pe.Fori(1, NGROUPS) as i:
                for n in range(SLOTS):
                    pe_slot("nodes", i, n, True)
            product_of("nodes", NGROUPS, -1)

        @block.vector
        def _(dve):
            v = nc.vector
            step = [0]

            def link(ins_):
                step[0] += 1
                ins_.then_inc(s_dve, 1)
                dve.wait_ge(s_dve, step[0])
                return step[0]

            v.memset(edge_in[:, 0, :], PAD_NODE).then_inc(s_ms, 1)
            v.memset(edge_in[:, 1, :], 0).then_inc(s_ms, 1)
            v.memset(ew_in[:, :], 0.0).then_inc(s_ms, 1)
            v.memset(b_three[:, :, :], 0.0).then_inc(s_ms, 1)
            v.memset(b_rows[:, :, :], 0.0)
            v.memset(ones_b[:, :], 1.0)
            v.memset(ones[:, :], 1.0)
            v.memset(ones_w[:, :], 1.0)
            v.memset(minus_half[:, :], -0.5)
            v.memset(eps_w[:, :], EPS)
            v.memset(half_w[:, :, :], -0.5)
            v.memset(src_before[:, :], -1.0)
            v.memset(sums[:, EG - 1, :], 0.0)
            v.memset(W_mask[:, :, :], 0.0)
            v.memset(counts[:, :, :], 0.0)
            v.memset(node_rec[:, :, :, :], 0.0)
            v.memset(rec[0][:, :, :], 0.0)
            v.memset(rec[1][:, :, :], 0.0)
            v.memset(none_row[:, :], 0.0)
            assert link(v.memset(zeros_b[:, :], 0.0)) == DVE_ZEROS
            dve.wait_ge(s_ms, 4)
            dve.wait_ge(s_ld, 16 * N_LOADS)
            dve.wait_ge(s_cst, 6)
            link(v.tensor_scalar(edge_lohi[:, 0, :], edge_in[:, 0, :], LO - 1, None, ALU.bitwise_and))
            link(v.tensor_scalar(edge_lohi[:, 1, :], edge_in[:, 0, :], 8, None, ALU.logical_shift_right))
            link(v.tensor_copy(edge_f[:, 0:2, :], edge_in[:, 0:2, :]))
            assert link(v.tensor_copy(edge_f[:, 2:4, :], edge_lohi[:, :, :])) == DVE_EDGE_F
            v.tensor_copy(count_b[:, :], count_f[:, :])
            dve.wait_ge(s_pe, 2)
            link(v.tensor_copy(cols[:, :, :].rearrange("p n t -> p (n t)"), banks[0][:, 0:5 * TILES]))
            assert link(v.tensor_copy(w_turn[:, :, :].rearrange("p c n -> p (c n)"), banks[1][:, :])) == DVE_W_TURN
            v.tensor_copy(W_av0[:, :, :].rearrange("p c n -> p (c n)"), banks[2][:, :])
            v.tensor_copy(W_av1[:, :, :].rearrange("p c n -> p (c n)"), banks[3][:, :])
            v.tensor_copy(cols_i[:, :, :], cols[:, 0:2, :])
            v.tensor_scalar(first_hi[:, :], cols[:, C_HI, :], 0.0, None, ALU.is_equal)
            link(v.tensor_scalar(dst_cut[:, :], cols[:, C_DST, :], float(LO), None, ALU.min))
            v.scalar_tensor_tensor(key[:, :], cols[:, C_SRC, :], float(LO + 1), dst_cut[:, :], ALU.mult, ALU.add)
            v.tensor_copy(to_spread[:, :, 0], cols[:, C_SRC, :])
            v.tensor_copy(to_spread[:, :, 2], cols[:, C_HI, :])
            link(v.tensor_copy(ew_b[:, 0, :], cols[:, C_EW, :]))
            v.tensor_copy(to_spread[:, :, 1], key[:, :])
            link(v.tensor_copy(ew_part[:, 0, :], ew_b[:, 0, :]))
            link(v.tensor_tensor(ew_rest[:, 0, :], cols[:, C_EW, :], ew_part[:, 0, :], ALU.subtract))
            link(v.tensor_copy(ew_b[:, 1, :], ew_rest[:, 0, :]))
            link(v.tensor_copy(ew_part[:, 1, :], ew_b[:, 1, :]))
            link(v.tensor_tensor(ew_rest[:, 1, :], ew_rest[:, 0, :], ew_part[:, 1, :], ALU.subtract))
            link(v.tensor_copy(ew_b[:, 2, :], ew_rest[:, 1, :]))
            link(v.tensor_copy(ew_part[:, 2, :], ew_b[:, 2, :]))
            link(v.tensor_copy(b_part[:, 0, :, :], b_three[:, :, :]))
            link(v.tensor_tensor(b_rest[:, :, :], b_three[:, :, :], b_part[:, 0, :, :], ALU.subtract))
            link(v.tensor_copy(b_part[:, 1, :, :], b_rest[:, :, :]))
            link(v.tensor_tensor(b_rest[:, :, :], b_rest[:, :, :], b_part[:, 1, :, :], ALU.subtract))
            link(v.tensor_copy(b_part[:, 2, :, :], b_rest[:, :, :]))
            for k in range(3):
                link(v.tensor_copy(b_rows[32 * k:32 * k + 1, :, :], b_part[32 * k:32 * k + 1, k, :, :]))
            dve.wait_ge(s_pe, 3)
            v.tensor_copy(W_gcn[:, :, :].rearrange("p c n -> p (c n)"), banks[4][:, :])
            v.tensor_tensor(b_gcn[:, :], banks[5][:, 0:2], b_cols[:, :, 1], ALU.add)
            link(v.scalar_tensor_tensor(none_row[:, D:2 * D], b_sum[0:1, :], ALPHA, b_sum[0:1, :],
                                        ALU.mult, ALU.max))
            assert step[0] == DVE_NONE_ROW == DVE_READY
            dve.wait_ge(s_pe, 4)
            dve.sem_inc(turn_hot_ready, 2)
            dve.sem_inc(hist_copied, 1)
            dve.sem_inc(mask_updated, 2)

            def column_of(array, t, n=None):
                return array[:, bass.ds(t, 1)] if n is None else array[:, n, bass.ds(t, 1)]

            def make_hot(t, q):
                dve.wait_ge(mask_updated, t + 1)
                v.tensor_scalar(oh_lo[:, q, :], count_b[:, :], column_of(cols, t, C_LO), None, ALU.is_equal)
                v.tensor_scalar(oh_hi[:, q, :], count_b[:, :], column_of(cols, t, C_HI), None, ALU.is_equal)
                for k in range(3):
                    v.tensor_scalar(oh_lo_w[:, q, k, :], count_b[:, :], column_of(cols, t, C_LO),
                                    column_of(ew_part, t, k), ALU.is_equal, ALU.mult)
                dve.wait_ge(spread_done, t + 1)
                v.scalar_tensor_tensor(junk[:, q, 0, 0:P], banks[q][:, P:2 * P], column_of(key, t), later[:, :],
                                       ALU.is_equal, ALU.mult,
                                       accum_out=again[:, q:q + 1]).then_inc(dup_counted, 1)
                for c in range(2):
                    v.tensor_scalar(oh_turn[:, q, c, :], banks[q][:, 2 * P:3 * P], part[:, c:c + 1],
                                    None, ALU.is_equal)
                v.scalar_tensor_tensor(junk[:, q, 0, P:2 * P], banks[q][:, 0:P], column_of(cols, t, C_SRC),
                                       earlier[:, :], ALU.is_equal, ALU.mult,
                                       accum_out=column_of(in_tile, t)).then_inc(turn_hot_ready, 1)
                dve.wait_ge(dup_counted, t + 1)
                v.tensor_scalar(keep[:, q:q + 1], again[:, q:q + 1], 0.0, column_of(first_hi, t),
                                ALU.is_equal, ALU.mult).then_inc(keep_ready, 1)
                dve.wait_ge(keep_ready, t + 1)
                v.tensor_scalar(oh_dst[:, q, :], count_b[:, :], column_of(cols, t, C_DST), keep[:, q:q + 1],
                                ALU.is_equal, ALU.mult).then_inc(oh_dst_ready, 1)

            def one_edge_tile(t, q, more):
                if more:
                    make_hot(t + 1, 1 - q)
                dve.wait_ge(look_done, t + 1)
                v.scalar_tensor_tensor(junk[:, q, 1, :], banks[2 + q][:, 0:LO], 1.0, oh_lo[:, q, :],
                                       ALU.mult, ALU.mult,
                                       accum_out=in_before[:, bass.ds(t, 1)])
                dve.wait_ge(weights_done, t + 1)
                dve.wait_ge(hits_copied, t + 1)
                dve.wait_ge(mask_updated, t + 2)
                dve.sem_inc(dve_past, 1)
                v.copy_predicated(W_mask[:, :, :].rearrange("p c n -> p (c n)"),
                                  hits[:, :].bitcast(U32), banks[4][:, :]).then_inc(mask_updated, 1)

            make_hot(0, 0)
            with dve.Fori(0, TILES // 2 - 1) as i:
                for q in range(2):
                    one_edge_tile(i * 2 + q, q, True)
            one_edge_tile(TILES - 2, 0, True)
            one_edge_tile(TILES - 1, 1, False)
            dve.wait_ge(mask_updated, TILES + 2)
            dve.wait_ge(hist_copied, TILES + 1)
            dve.wait_ge(hist_done, TILES)
            link(v.tensor_tensor(place[:, :], in_tile[:, :], in_before[:, :], ALU.add))
            for c in range(2):
                v.tensor_tensor_scan(scan[:, c, :], ones_w[:, :], counts[:, c, :], 0.0, ALU.mult, ALU.add)
            wdeg, ok, root, rest = (tmp[:, n, :, :] for n in range(4))
            link(v.tensor_scalar(wdeg, banks[7][:, :].rearrange("p (c l) -> p c l", c=2), 1.0, None, ALU.add))
            assert step[0] == DVE_SCAN
            link(v.tensor_scalar(ok, wdeg, 0.0, None, ALU.is_gt))
            link(v.tensor_scalar(wdeg, wdeg, 1e-30, None, ALU.max))


            def inverse_root(to, of, aside):
                link(v.reciprocal(to, to))
                link(v.scalar_tensor_tensor(aside, to, -0.5, to, ALU.mult, ALU.mult))
                link(v.tensor_tensor(aside, aside, of, ALU.mult))
                link(v.scalar_tensor_tensor(to, aside, 1.5, to, ALU.add, ALU.mult))

            dve.wait_ge(s_roots, 1)
            inverse_root(root, wdeg, rest)
            link(v.tensor_tensor(node_rec[:, :, :, N_DINV], root, ok, ALU.mult))
            v.tensor_tensor(node_rec[:, :, :, N_DINV2], node_rec[:, :, :, N_DINV],
                            node_rec[:, :, :, N_DINV], ALU.mult)
            dve.wait_ge(s_pe, 5)
            v.tensor_copy(base[:, 0:1], banks[0][:, 0:1])
            link(v.tensor_copy(base[:, 1:2], banks[0][:, 1:2]))
            link(v.tensor_tensor(base[:, 1:2], base[:, 1:2], banks[1][:, 0:1], ALU.add))
            for c in range(2):
                link(v.tensor_scalar(scan[:, c, :], scan[:, c, :], base[:, c:c + 1], None, ALU.add))
            link(v.tensor_tensor(node_rec[:, :, :, N_START], scan[:, :, :], counts[:, :, :], ALU.subtract))
            link(v.tensor_scalar(ok, counts[:, :, :], 0.0, None, ALU.is_gt))
            link(v.scalar_tensor_tensor(rest, scan[:, :, :], -1.0 - NONE, ok, ALU.add, ALU.mult))
            link(v.tensor_scalar(node_rec[:, :, :, N_LASTF], rest, float(NONE), None, ALU.add))
            v.tensor_copy(node_rec[:, :, :, N_LAST].bitcast(I32), node_rec[:, :, :, N_LASTF])
            link(v.tensor_scalar(rest, counts[:, :, :], 1.0, None, ALU.max))
            v.reciprocal(node_rec[:, :, :, N_MEAN], rest)
            dve.wait_ge(s_roots, 2)
            inverse_root(wdeg, rest, root)
            link(v.tensor_tensor(node_rec[:, :, :, N_WINV], wdeg, ok, ALU.mult))
            assert step[0] == DVE_NODE_REC

            def pick_ends(i, h):
                for n in range(2):
                    v.tensor_copy(idx2[h][:, n, :],
                                  cols_i[:, n, bass.ds(i * (2 * BG) + h * BG, BG)]).then_inc(idx_ready[h], 1)

            def make_records(i, h, first=False):
                at = bass.ds(i * (2 * BG) + h * BG, BG)
                to, s_, d_ = rec[h], ns[h], nd[h]
                if not first:
                    dve.wait_ge(rec_scattered[h], i * (16 * BG))
                dve.wait_ge(ends_gathered[h], i * (32 * BG) + 32 * BG)
                v.tensor_copy(to[:, :, R_SRC], cols[:, C_SRC, at])
                v.tensor_copy(to[:, :, R_DST].bitcast(I32), cols[:, C_DST, at])
                v.tensor_tensor(rec_at[h][:, :], s_[:, :, N_START], place[:, at], ALU.add)
                v.tensor_copy(to[:, :, R_LAST].bitcast(I32), d_[:, :, N_LASTF])
                v.tensor_tensor(to[:, :, R_C2], s_[:, :, N_WINV], d_[:, :, N_WINV], ALU.mult)
                v.tensor_copy(to[:, :, R_C3], s_[:, :, N_MEAN])
                v.tensor_copy(to[:, :, R_SELF], d_[:, :, N_DINV2])
                v.tensor_tensor(to[:, :, R_C1], s_[:, :, N_DINV], d_[:, :, N_DINV],
                                ALU.mult).then_inc(rec_step[h], 1)
                dve.wait_ge(rec_step[h], i + 1)
                v.tensor_tensor(to[:, :, R_C1], to[:, :, R_C1], cols[:, C_EW, at],
                                ALU.mult).then_inc(rec_ready[h], 1)

            pick_ends(0, 0)
            pick_ends(0, 1)
            for h in range(2):
                make_records(0, h, True)
                pick_ends(1, h)
            with dve.Fori(1, BGROUPS // 2 - 1) as i:
                for h in range(2):
                    make_records(i, h)
                    pick_ends(i + 1, h)
            for h in range(2):
                make_records(BGROUPS // 2 - 1, h)

            def source(ph, n):
                n %= MEASURED[ph] * pairs(ph)
                stage, j = divmod(n, pairs(ph))
                ring = prod_ring(ph)
                k = n - pairs(ph)
                for t in range(2):
                    g = 2 * j + t
                    if (ph, stage) in (("edges4", 1), ("nodes", 3)):
                        yield g, ring[k % len(ring)][:, t * D:t * D + D]
                    elif stage == 0 and ph != "edges3":
                        yield g, rows[:, g, :]
                    elif (ph, stage) == ("nodes", 2):
                        yield g, resid3[:, g, :]
                    else:
                        yield g, resid[:, g, :]

            def add(ph, i, n):
                stage, j = divmod(n, pairs(ph))
                a, b = 2 * j, 2 * j + 2
                ring = prod_ring(ph)
                k = n - pairs(ph)
                from_bank = ring[k % len(ring)][:, :].rearrange("p (t f) -> p t f", f=D)
                if (ph, stage) in (("edges1", 1), ("edges2", 1), ("nodes", 1)):
                    if ph != "nodes":
                        dve.wait_ge(resid_stored.sem, resid_stored.at(ph, i, -1))
                    dve.wait_ge(product.sem, product.at(ph, i, k))
                    v.tensor_tensor(resid[:, a:b, :], from_bank, rows[:, a:b, :],
                                    ALU.add).then_inc(resid_ready.sem, 1)
                if (ph, stage) == ("edges3", 0):
                    dve.wait_ge(resid_stored.sem, resid_stored.at(ph, i, -1))
                    v.tensor_tensor(resid[:, a:b, :], rows[:, a:b, :], got_e[:, a:b, :],
                                    ALU.add).then_inc(resid_ready.sem, 1)
                if (ph, stage) == ("nodes", 2):
                    dve.wait_ge(skip_ready.sem, skip_ready.at(ph, i, j))
                    dve.wait_ge(product.sem, product.at(ph, i, k))
                    v.tensor_tensor(resid3[:, a:b, :], from_bank, skip[:, a:b, :],
                                    ALU.add).then_inc(resid_ready.sem, 1)

            def measure(ph, i, n):
                stage, j = divmod(n, pairs(ph))
                if (ph, stage) in (("edges1", 1), ("edges2", 1), ("edges3", 0), ("nodes", 1)):
                    dve.wait_ge(resid_ready.sem, resid_ready.at(ph, i, j))
                if (ph, stage) == ("nodes", 2):
                    dve.wait_ge(resid_ready.sem, resid_ready.at(ph, i, NPAIR + j))
                if (ph, stage) in (("edges4", 1), ("nodes", 3)):
                    dve.wait_ge(product.sem, product.at(ph, i, n - pairs(ph)))
                for g, rows_ in source(ph, n):
                    last = v.bn_stats(stats[:, g, :], rows_)
                last.then_inc(stats_done.sem, 1)

            def aggregate(ph, i, n):
                dve.wait_ge(stats_done.sem, stats_done.at(ph, i, n))
                dve.sem_inc(dve_past, 1)
                for g, _ in source(ph, n):
                    last = v.bn_aggr(moments[:, g, :], stats[:, g, :])
                last.then_inc(moments_ready.sem, 1)

            def normalise(ph, i, n):
                if ph != "nodes" and n < EP:
                    dve.wait_ge(summed.sem, summed.at(ph, i, 2 * n + 1 - EG))
                dve.wait_ge(rstd_ready.sem, rstd_ready.at(ph, i, n))
                for g, rows_ in source(ph, n):
                    last = v.tensor_scalar(left[:, g, :], rows_, moments[:, g, 0:1],
                                           rstd[:, g:g + 1], ALU.subtract, ALU.mult)
                last.then_inc(normed.sem, 1)

            def relu_plus(ph, i, n, gathered_rows):
                stage, j = divmod(n, pairs(ph))
                a, b = 2 * j, 2 * j + 2
                dve.wait_ge(normed.sem, normed.at(ph, i, n))
                v.scalar_tensor_tensor(left[:, a:b, :], left[:, a:b, :], 0.0, gathered_rows[:, a:b, :],
                                       ALU.max, ALU.add).then_inc(plus_ready.sem, 1)

            def relu_message(ph, i, n, coef):
                dve.wait_ge(normed.sem, normed.at(ph, i, n))
                for g, _ in source(ph, n):
                    last = v.tensor_scalar(left[:, g, :], left[:, g, :], 0.0, rec_now[:, g, coef:coef + 1],
                                           ALU.max, ALU.mult)
                last.then_inc(message_ready.sem, 1)

            def product_message(ph, i, j, coef):
                ring = prod_ring(ph)
                k = EP + j
                dve.wait_ge(product.sem, product.at(ph, i, k))
                for t in range(2):
                    g = 2 * j + t
                    last = v.tensor_scalar(left[:, g, :], ring[k % len(ring)][:, t * D:t * D + D],
                                           rec_now[:, g, coef:coef + 1], None, ALU.mult)
                last.then_inc(message_ready.sem, 1)

            def compare_sources(ph, i, j):
                dve.wait_ge(summed.sem, summed.at(ph, i, 2 * j + 1 - EG))
                dve.wait_ge(src_spread.sem, src_spread.at(ph, i, j))
                for t in range(2):
                    g = 2 * j + t
                    spread = spread_bank[:, t * P:t * P + P]
                    v.tensor_scalar(same[:, g, :], spread, rec_now[:, g, R_SRC:R_SRC + 1], None, ALU.is_equal)
                    before = rec_now[:, g - 1, R_SRC:R_SRC + 1] if g else src_before[:, :]
                    last = v.tensor_scalar(goes_on[:, g, :], spread, before, is_last[:, :],
                                           ALU.is_equal, ALU.mult)
                last.then_inc(same_ready.sem, 1)

            COEF = {"edges1": R_C1, "edges2": R_C2, "edges3": R_C3, "edges4": R_C3}
            COMPARE_AFTER, MESSAGE_AFTER = 5, 6

            def edges_slot(ph, i, n):
                steps = MEASURED[ph] * EP
                if n < steps:
                    add(ph, i, n)
                    measure(ph, i, n)
                if 1 <= n <= steps:
                    normalise(ph, i, n - 1)
                if n < steps:
                    aggregate(ph, i, n)
                if 1 <= n <= steps:
                    if ph in ("edges2", "edges4") and n - 1 < EP:
                        relu_plus(ph, i, n - 1, got_e)
                    if (ph, (n - 1) // EP) in (("edges1", 1), ("edges3", 0)):
                        relu_message(ph, i, n - 1, COEF[ph])
                if 0 <= n - COMPARE_AFTER < EP:
                    compare_sources(ph, i, n - COMPARE_AFTER)
                if ph in ("edges2", "edges4") and 0 <= n - EP - MESSAGE_AFTER < EP:
                    product_message(ph, i, n - EP - MESSAGE_AFTER, COEF[ph])

            for ph, passes in PHASES[:-1]:
                if ph != "edges1":
                    dve.wait_ge(src_kept.sem, src_kept.all(f"edges{int(ph[-1]) - 1}"))
                    v.memset(src_before[:, :], -1.0)
                with dve.Fori(0, passes) as i:
                    dve.wait_ge(src_kept.sem, src_kept.at(ph, i, -1))
                    dve.wait_ge(rec_loaded.sem, rec_loaded.at(ph, i, 0))
                    v.tensor_copy(rec_now[:, :, :].rearrange("p t f -> p (t f)"),
                                  rec_land[:, :]).then_inc(work_ready.sem, 1)
                    dve.wait_ge(work_ready.sem, work_ready.at(ph, i, 0))
                    if ph != "edges1":
                        dve.wait_ge(rows_loaded.sem, rows_loaded.at(ph, i, 0))
                    dve.wait_ge(gathered.sem, gathered.at(ph, i, EG - 1))
                    for n in range(2 * EP + MESSAGE_AFTER):
                        edges_slot(ph, i, n)
                    if ph == "edges2":
                        dve.wait_ge(table_stored.sem, table_stored.at(ph, i, -1))
                        for j in range(EP):
                            for g in (2 * j, 2 * j + 1):
                                dve.wait_ge(sums_copied.sem, sums_copied.at(ph, i, g))
                                last = v.tensor_tensor(pre[:, g, :], sums[:, g, :], b_sum[:, :], ALU.add)
                            last.then_inc(biased.sem, 1)
                        for j in range(EP):
                            a, b = 2 * j, 2 * j + 2
                            dve.wait_ge(biased.sem, biased.at(ph, i, j))
                            v.scalar_tensor_tensor(pre[:, a:b, :], pre[:, a:b, :], ALPHA, pre[:, a:b, :],
                                                   ALU.mult, ALU.max).then_inc(leaky_ready.sem, 1)
                    dve.wait_ge(same_ready.sem, same_ready.at(ph, i, EP - 1))
                    v.tensor_copy(src_before[:, :], rec_now[:, EG - 1, R_SRC:R_SRC + 1]).then_inc(src_kept.sem, 1)

            ph = "nodes"

            def nodes_slot(i, n, main, before):
                s, j = divmod(n, NPAIR)
                if main and n == 0:
                    dve.wait_ge(rec_loaded.sem, rec_loaded.at(ph, i, 0))
                    v.tensor_copy(node_now[:, :, :].rearrange("p t f -> p (t f)"),
                                  node_land[:, :]).then_inc(work_ready.sem, 1)
                if before and s == 0:
                    a, b, k = 2 * j, 2 * j + 2, 3 * NPAIR + j
                    ring = prod_ring(ph)
                    if j == 0:
                        dve.wait_ge(out_stored.sem, out_stored.at(ph, i, -2))
                    dve.wait_ge(product.sem, product.at(ph, i, k - SLOTS))
                    v.tensor_tensor(pre[:, a:b, :], ring[k % len(ring)][:, :].rearrange("p (t f) -> p t f", f=D),
                                    got[:, a:b, 3 * D:4 * D], ALU.add).then_inc(pre_ready.sem, 1)
                m = pair_at(n, 6)
                if before and m is not None:
                    a, b = 2 * m, 2 * m + 2
                    dve.wait_ge(silu_ready.sem, silu_ready.at(ph, i, m - NPAIR))
                    v.tensor_tensor(pre[:, a:b, :], resid3[:, a:b, :], pre[:, a:b, :],
                                    ALU.add).then_inc(out_ready.sem, 1)
                if main:
                    add(ph, i, n)
                m = pair_at(n, 1)
                if before and m is not None:
                    dve.wait_ge(pre_ready.sem, pre_ready.at(ph, i, m - NPAIR))
                    for g in (2 * m, 2 * m + 1):
                        last = v.bn_stats(stats_l[:, g, :], pre[:, g, :])
                    last.then_inc(stats_done_l.sem, 1)
                if main:
                    if n == 0:
                        dve.wait_ge(rows_loaded.sem, rows_loaded.at(ph, i, 0))
                    measure(ph, i, n)
                if n > 0 and main or n == 0 and before:
                    normalise(ph, i, n - 1)
                if main:
                    aggregate(ph, i, n)
                if before and m is not None:
                    dve.wait_ge(stats_done_l.sem, stats_done_l.at(ph, i, m - NPAIR))
                    dve.sem_inc(dve_past, 1)
                    for g in (2 * m, 2 * m + 1):
                        last = v.bn_aggr(moments_l[:, g, :], stats_l[:, g, :])
                    last.then_inc(moments_ready_l.sem, 1)
                if main and 1 <= n and (n - 1) // NPAIR in (1, 2):
                    if n - 1 == NPAIR:
                        dve.wait_ge(gathered.sem, gathered.at(ph, i, NG - 1))
                    relu_plus(ph, i, n - 1, got[:, :, 0:D] if (n - 1) // NPAIR == 1 else got[:, :, 2 * D:3 * D])
                m = pair_at(n, 2)
                if before and m is not None:
                    dve.wait_ge(rstd_ready_l.sem, rstd_ready_l.at(ph, i, m - NPAIR))
                    for g in (2 * m, 2 * m + 1):
                        last = v.tensor_scalar(pre[:, g, :], pre[:, g, :], moments_l[:, g, 0:1],
                                               rstd_l[:, g:g + 1], ALU.subtract, ALU.mult)
                    last.then_inc(normed_l.sem, 1)

            dve.wait_ge(table_stored.sem, table_stored.all("edges4"))
            dve.wait_ge(summed.sem, summed.all("edges4"))
            for n in range(SLOTS):
                nodes_slot(0, n, True, False)
            with dve.Fori(1, NGROUPS) as i:
                for n in range(SLOTS):
                    nodes_slot(i, n, True, True)
            for n in range(SLOTS):
                nodes_slot(NGROUPS, n, False, True)


_INS = ["x", "src", "dst", "edge_weight", "L1_gnn_W", "L1_gnn_b", "L1_gnn_W1", "L1_gnn_b1", "L1_gnn_W2", "L1_gnn_b2",
        "L2_gnn_W", "L2_gnn_b", "L3_gnn_W0", "L3_gnn_b0", "L3_gnn_g0", "L3_gnn_beta0", "L3_gnn_W1", "L3_gnn_b1",
        "L3_gnn_g1", "L3_gnn_beta1"]
_SCRATCH = {"node_tab": ((HI * LO, NF), F32), "rec_sorted": ((TILES * P, RF), F32),
            "rec_groups": ((EGROUPS, P, EG * RF), F32), "state": ((EGROUPS, P, EG, D), F32),
            "table": ((TILES * P + 1, 4 * D), F32), "column0": ((TILES * P + 1, D), F32), "column1": ((TILES * P + 1, D), F32),
            "column2": ((TILES * P + 1, D), F32), "begin": ((2, D), F32)}


def kernel(**inputs):
    import numpy as _np
    import concourse.bacc as _bacc
    from concourse.bass_utils import run_bass_kernel_spmd as _run

    nc = _bacc.Bacc("TRN2", target_bir_lowering=False, num_devices=1)
    arrays, args = {}, {}
    for name in _INS:
        a = _np.ascontiguousarray(inputs[name])
        arrays[f"in_{name}"] = a
        args[name] = nc.dram_tensor(f"in_{name}", a.shape, mybir.dt.from_np(a.dtype), kind="ExternalInput").ap()
    out = nc.dram_tensor("out", (NODES, D), F32, kind="ExternalOutput").ap()
    scratch = {n: nc.dram_tensor(n, shape, dt).ap() for n, (shape, dt) in _SCRATCH.items()}
    gnn_stack(nc, args, out, scratch)
    r = _run(nc, [arrays], core_ids=[0])
    return r.results[0]["out"]
```

```python
from contextlib import ExitStack

import numpy as np

import concourse.bass as bass
from concourse import mybir

P = 128
D = 256
NODES = 50000
EDGES = 12500
LO = 256
HI = 256
TILES = -(-EDGES // P)
EG = 14
EGROUPS = TILES // EG
NG = 12
NROWS = NG * P
NGROUPS = -(-NODES // NROWS)
LAST = NODES - NROWS
EP, NPAIR = EG // 2, NG // 2
HALF = 2 * ((EP + 1) // 2)
HALVES = [(0, HALF), (HALF, EG)]
BG = 7
BGROUPS = TILES // BG
NONE = TILES * P
PAD_NODE = HI * LO - 1
NF = 8
N_START, N_LAST, N_DINV, N_DINV2, N_WINV, N_MEAN, N_LASTF = range(7)
RF = 8
R_SRC, R_DST, R_LAST, R_C1, R_C2, R_C3, R_SELF = range(7)
EPS = 1e-5
ALPHA = 0.2

F32 = mybir.dt.float32
BF16 = mybir.dt.bfloat16
I32 = mybir.dt.int32
U32 = mybir.dt.uint32
ALU = mybir.AluOpType
ACT = mybir.ActivationFunctionType

PHASES = [("edges1", EGROUPS), ("edges2", EGROUPS), ("edges3", EGROUPS), ("edges4", EGROUPS),
          ("nodes", NGROUPS)]


class Signal:

    def __init__(self, sem, before, per, step=1):
        self.sem, self.per, self.base, self.step = sem, dict(zip([p for p, _ in PHASES], per)), {}, step
        n = before
        for name, passes in PHASES:
            self.base[name] = n
            n += self.per[name] * passes
        self.total = n

    def at(self, phase, i, k):
        return (i * self.per[phase] + (self.base[phase] + k + 1)) * self.step

    def all(self, phase):
        passes = dict(PHASES)[phase]
        return (self.base[phase] + self.per[phase] * passes) * self.step


def gnn_stack(nc, ins, out, scratch):
    x = ins["x"]
    node_tab, rec_sorted = scratch["node_tab"], scratch["rec_sorted"]
    state, table = scratch["state"], scratch["table"]
    column = [scratch[f"column{k}"] for k in range(3)]

    with ExitStack() as ctx:
        def sb(name, shape, dt=F32):
            return ctx.enter_context(nc.sbuf_tensor(name, shape, dt))

        def sem(name):
            return ctx.enter_context(nc.semaphore(name))

        bank = [ctx.enter_context(nc.psum_tensor(f"bank{j}", [P, 512], F32)) for j in range(8)]
        sum_bank, spread_bank = bank[5:7], bank[7]

        def turn_ring(ph):
            return bank[0:3] if ph == "nodes" else bank[0:2]

        def prod_ring(ph):
            return bank[3:8] if ph == "nodes" else bank[2:5]

        ident = sb("ident", [P, P])
        earlier = sb("earlier", [P, P])
        later = sb("later", [P, P])
        ones = sb("ones", [P, P])
        ones_b = sb("ones_b", [P, P], BF16)
        zeros_b = sb("zeros_b", [P, 512], BF16)
        count_f = sb("count_f", [P, LO])
        count_b = sb("count_b", [P, LO], BF16)
        part = sb("part", [P, 2])
        is_last = sb("is_last", [P, 1])
        minus_half = sb("minus_half", [P, EG])
        eps_w = sb("eps_w", [P, EG])
        W_mask = sb("W_mask", [P, 2, D])
        W_gcn = sb("W_gcn", [P, 2, D])
        W_head = sb("W_head", [P, 2, D])
        W_sum = sb("W_sum", [P, 2, D])
        W_av0 = sb("W_av0", [P, 2, D])
        W_av1 = sb("W_av1", [P, 2, D])
        b_cols = sb("b_cols", [P, 2, 4])
        b_gcn = sb("b_gcn", [P, 2])
        b_rows = sb("b_rows", [P, 3, D], BF16)
        b_sum = sb("b_sum", [P, D])
        g_last = sb("g_last", [P, D])
        beta_last = sb("beta_last", [P, D])
        none_row = sb("none_row", [1, 4 * D])

        rec_land = sb("rec_land", [P, EG * RF])
        rec_now = sb("rec_now", [P, EG, RF])
        node_land = sb("node_land", [P, NG * NF])
        node_now = sb("node_now", [P, NG, NF])
        rec_before = sb("rec_before", [P, EG, RF])
        rows = sb("rows", [P, EG, D])
        resid = sb("resid", [P, EG, D])
        resid3 = sb("resid3", [P, NG, D])
        left = sb("left", [P, EG, D])
        turned = sb("turned", [P, EG, D])
        hidden = sb("hidden", [P, 2, EG, P])
        skip = sb("skip", [P, NG, D])

        home = [b_[:, :, :].rearrange("p t f -> p (t f)") for b_ in (resid, left, turned, resid3, skip)]
        room = [EG * D, EG * D, EG * D, NG * D, NG * D]
        taken = [0] * 5

        def early(name, shape, dt=F32):
            size = int(np.prod(shape[1:]))
            words = size // 2 if dt == BF16 else size
            words += words % 2
            k = next(k for k in range(5) if taken[k] + words <= room[k])
            flat = home[k][0:shape[0], taken[k]:taken[k] + words]
            taken[k] += words
            if dt != F32:
                flat = flat.bitcast(dt)
            flat = flat[:, 0:size]
            if len(shape) == 2:
                return flat
            dims = "abcd"[:len(shape) - 1]
            return flat.rearrange(f"p ({' '.join(dims)}) -> p {' '.join(dims)}",
                                  **{d: n for d, n in zip(dims, shape[1:])})

        b_part = early("b_part", [P, 3, 3, D], BF16)
        b_rest = early("b_rest", [P, 3, D])
        b_three = early("b_three", [P, 3, D])
        w_turn = early("w_turn", [P, 2, D])
        edge_in = early("edge_in", [TILES, 3, P], I32)
        ew_in = early("ew_in", [TILES, P])
        edge_lohi = early("edge_lohi", [TILES, 2, P], I32)
        edge_f = early("edge_f", [TILES, 4, P])
        cols = early("cols", [P, 5, TILES])
        C_SRC, C_DST, C_LO, C_HI, C_EW = range(5)
        cols_i = early("cols_i", [P, 2, TILES], I32)
        key = early("key", [P, TILES])
        to_spread = early("to_spread", [P, TILES, 3])
        spread_now = early("spread_now", [P, 2, 3])
        dst_cut = early("dst_cut", [P, TILES])
        first_hi = early("first_hi", [P, TILES])
        ew_part = early("ew_part", [P, 3, TILES])
        ew_b = early("ew_b", [P, 3, TILES], BF16)
        ew_rest = early("ew_rest", [P, 2, TILES])
        in_tile = early("in_tile", [P, TILES])
        in_before = early("in_before", [P, TILES])
        place = early("place", [P, TILES])
        oh_lo = early("oh_lo", [P, 2, LO], BF16)
        oh_hi = early("oh_hi", [P, 2, HI], BF16)
        oh_lo_w = early("oh_lo_w", [P, 2, 3, LO], BF16)
        oh_dst = early("oh_dst", [P, 2, LO], BF16)
        oh_dst_w = early("oh_dst_w", [P, 2, 3, LO], BF16)
        oh_turn = early("oh_turn", [P, 2, 2, P])
        junk = early("junk", [P, 2, 2, LO], BF16)
        again = early("again", [P, 2])
        keep = early("keep", [P, 2])
        hits = early("hits", [P, 512])
        counts = early("counts", [P, 2, LO])
        scan = early("scan", [P, 2, LO])
        ones_w = early("ones_w", [P, LO])
        base = early("base", [P, 2])
        idx2 = [early(f"idx2_{h}", [P, 2, BG], I32) for h in range(2)]
        ns = [early(f"ns_{h}", [P, BG, NF]) for h in range(2)]
        nd = [early(f"nd_{h}", [P, BG, NF]) for h in range(2)]
        rec = [early(f"rec_{h}", [P, BG, RF]) for h in range(2)]
        rec_at = [early(f"rec_at_{h}", [P, BG], I32) for h in range(2)]


        pre = sb("pre", [P, EG, D])
        got = sb("got", [P, NG, 4 * D])
        got_flat = got[:, :, :].rearrange("p t f -> p (t f)")

        def at_got(start, n, shape, **sizes):
            return got_flat[:, start:start + n].rearrange(shape, **sizes)

        got_e = at_got(0, EG * D, "p (t f) -> p t f", f=D)
        sums = at_got(EG * D, EG * D, "p (t f) -> p t f", f=D)
        same = at_got(2 * EG * D, EG * P, "p (t f) -> p t f", f=P)
        goes_on = at_got(2 * EG * D + EG * P, EG * P, "p (t f) -> p t f", f=P)

        def message(g):
            return skip[:, g, :] if g < NG else resid3[:, g - NG, :]

        node_rec = at_got(0, 2 * LO * NF, "p (c l f) -> p c l f", c=2, l=LO)
        w_in = hidden[:, :, :, :].rearrange("p c t r -> p (c t r)")[:, 0:8 * D].rearrange(
            "p (w c n) -> p w c n", w=4, c=2)
        tmp = pre[:, :, :].rearrange("p t f -> p (t f)")[:, 0:8 * LO].rearrange(
            "p (n c l) -> p n c l", n=4, c=2)
        stats = sb("stats", [P, EG, 6])
        moments = sb("moments", [P, EG, 2])
        var_eps = sb("var_eps", [P, EG])
        rstd = sb("rstd", [P, EG])
        stats_l = sb("stats_l", [P, NG, 6])
        moments_l = sb("moments_l", [P, NG, 2])
        var_eps_l = sb("var_eps_l", [P, NG])
        rstd_l = sb("rstd_l", [P, NG])

        EDGE_LOADS, WEIGHT_LOADS = 6, 26
        DVE_ZEROS, DVE_EDGE_F, DVE_READY = 1, 5, 15
        DVE_SCAN, DVE_ROOT1, DVE_ROOT2, DVE_NODE_REC = 17, 19, 33, 38
        DVE_W_TURN, DVE_NONE_ROW = 39, 48

        dve_past, pool_past = sem("dve_past"), sem("pool_past")
        s_ld = sem("edges_loaded")
        s_ld_w = sem("weights_loaded")
        s_ms = sem("pads_set")
        s_cst = sem("constants_set")
        s_pool = sem("pool_setup_step")
        s_dve = sem("dve_setup_step")
        s_pe = sem("pe_setup_step")
        s_roots = sem("roots_ready")
        cols_picked = sem("cols_picked")
        spread_done = sem("spread_done")
        turn_hot_ready = sem("turn_hot_ready")
        hot_ready = sem("hot_ready")
        dup_counted = sem("dup_counted")
        keep_ready = sem("keep_ready")
        oh_dst_ready = sem("oh_dst_ready")
        oh_lo_ready = sem("oh_lo_ready")
        lo_weighted = sem("lo_weighted")
        look_done = sem("look_done")
        hist_done = sem("hist_done")
        hist_copied = sem("hist_copied")
        pairs_done = sem("pairs_done")
        weights_done = sem("weights_done")
        hits_copied = sem("hits_copied")
        mask_updated = sem("mask_updated")
        node_stored = sem("node_records_stored")
        idx_ready = [sem("idx_ready_even"), sem("idx_ready_odd")]
        ends_gathered = [sem("ends_gathered_even"), sem("ends_gathered_odd")]
        rec_step = [sem("rec_step_even"), sem("rec_step_odd")]
        rec_ready = [sem("rec_ready_even"), sem("rec_ready_odd")]
        rec_scattered = [sem("rec_scattered_even"), sem("rec_scattered_odd")]

        E, N = EP, NPAIR
        PRIME = 32
        S = lambda name, per, before=PRIME, step=1: Signal(sem(name), before, per, step)
        rec_loaded = S("rec_loaded", [1, 1, 1, 1, 1], 0, 16)
        work_ready = S("work_ready", [1, 1, 1, 1, 1])
        rows_loaded = [S("rows_loaded", [0, 1, 1, 1, 1], 0, 16), S("rows_loaded_rest", [0, 1, 1, 1, 0], 0, 16)]
        gathered = [S("gathered", [HALF, HALF, HALF, HALF, NG], 0, 16),
                    S("gathered_rest", [EG - HALF] * 4 + [0], 0, 16)]
        stats_done = S("stats_done", [2 * E, 2 * E, E, 2 * E, 4 * N])
        moments_ready = S("moments_ready", [2 * E, 2 * E, E, 2 * E, 4 * N])
        eps_added = S("eps_added", [2 * E, 2 * E, E, 2 * E, 4 * N])
        rstd_raw = S("rstd_raw", [0, E, 0, 0, N])
        rstd_ready = S("rstd_ready", [2 * E, 2 * E, E, 2 * E, 4 * N])
        normed = S("normed", [2 * E, 2 * E, E, 2 * E, 4 * N])
        plus_ready = S("plus_ready", [0, E, 0, E, 2 * N])
        turn_done = S("turn_done", [E, 2 * E, 0, 2 * E, 4 * N])
        turned_ready = S("turned_ready", [E, 2 * E, 0, 2 * E, 4 * N])
        hidden_done = S("hidden_done", [0, E, 0, 0, N])
        hidden_ready = S("hidden_ready", [0, E, 0, 0, N])
        product = S("product", [E, 2 * E, 0, 2 * E, 4 * N])
        resid_ready = S("resid_ready", [E, E, E, 0, 2 * N])
        resid_stored = [S(f"resid_stored{r}", [1, 1, 1, 0, 0], 1, 16) for r in ("", "_rest")]
        src_spread = S("src_spread", [(E + 1) // 2] * 4 + [0])
        same_ready = S("same_ready", [E, E, E, E, 0])
        rec_kept = S("rec_kept", [1, 1, 1, 1, 0])
        message_ready = S("message_ready", [E, E, E, E, 0])
        summed = S("summed", [EG, EG, EG, EG, 0])
        sums_copied = S("sums_copied", [EG, EG, EG, EG, 0])
        biased = S("biased", [0, E, 0, 0, 0])
        leaky_ready = S("leaky_ready", [0, E, 0, 0, 0])
        table_stored = [S(f"table_stored{r}", [1, 1, 1, 1, 0], 1, 16) for r in ("", "_rest")]
        column_stored = [S("column_stored", [1, 1, 1, 0, 0], 3, 16), S("column_stored_rest", [1, 1, 1, 0, 0], 1, 16)]
        skip_ready = S("skip_ready", [0, 0, 0, 0, N])
        pre_ready = S("pre_ready", [0, 0, 0, 0, N])
        stats_done_l = S("stats_done_l", [0, 0, 0, 0, N])
        moments_ready_l = S("moments_ready_l", [0, 0, 0, 0, N])
        eps_added_l = S("eps_added_l", [0, 0, 0, 0, N])
        rstd_ready_l = S("rstd_ready_l", [0, 0, 0, 0, N])
        gained = S("gained", [0, 0, 0, 0, N])
        shifted = S("shifted", [0, 0, 0, 0, N])
        silu_ready = S("silu_ready", [0, 0, 0, 0, N])
        out_ready = S("out_ready", [0, 0, 0, 0, N])
        out_stored = S("out_stored", [0, 0, 0, 0, 1], 1, 16)
        primed = [work_ready, stats_done, moments_ready, eps_added, rstd_raw, rstd_ready, normed, plus_ready,
                  turn_done, turned_ready, hidden_done, hidden_ready, product, resid_ready,
                  src_spread, same_ready, rec_kept, message_ready, summed, sums_copied, biased, leaky_ready,
                  skip_ready, pre_ready, stats_done_l, moments_ready_l, eps_added_l, rstd_ready_l,
                  gained, shifted, silu_ready, out_ready]

        MEASURED = {"edges1": 2, "edges2": 2, "edges3": 1, "edges4": 2, "nodes": 4}
        TURNED = {"edges1": 1, "edges2": 2, "edges3": 0, "edges4": 2, "nodes": 4}
        HIDDEN = {"edges2": 0, "nodes": 1}

        SLOTS = 4 * NPAIR

        def pair_at(n, k):
            return (n - k) // 2 if n >= k and (n - k) % 2 == 0 and (n - k) // 2 < NPAIR else None

        def steps(ph):
            return MEASURED[ph] * pairs(ph)

        def compare_slot(ph, j):
            return min(j + 1, EP - 1) if ph == "edges3" else j + COMPARE_AFTER

        def adding(ph, i, n, main, before):
            j = n - ADD_AFTER[ph] if n < steps(ph) else EP
            if main and 0 <= j < EP:
                yield i, j
            j = n + steps(ph) - ADD_AFTER[ph]
            if before and 0 <= j < EP:
                yield i - 1, j

        def spread_slot(ph, q):
            return 2 * q if ph == "edges3" else 2 * q + SPREAD_AFTER

        SPREAD_AFTER, COMPARE_AFTER, MESSAGE_AFTER = 1, 5, 6
        ADD_AFTER = {"edges1": EP + 3, "edges2": 2 * EP, "edges3": 2, "edges4": 2 * EP}

        def pairs(ph):
            return NPAIR if ph == "nodes" else EP

        def rows_to_turn(ph, i, n):
            stage, j = divmod(n, pairs(ph))
            plus = {"edges2": [0], "edges4": [0], "nodes": [1, 2]}.get(ph, [])
            if stage in plus:
                return plus_ready.sem, plus_ready.at(ph, i, plus.index(stage) * pairs(ph) + j)
            return normed.sem, normed.at(ph, i, n)

        def product_read(ph, i, k, back):
            stage, j = divmod(k, pairs(ph))
            by = {("edges1", 0): (resid_ready, j), ("edges2", 0): (resid_ready, j),
                  ("edges2", 1): (message_ready, j), ("edges4", 0): (normed, EP + j),
                  ("edges4", 1): (message_ready, j), ("nodes", 0): (resid_ready, j),
                  ("nodes", 1): (resid_ready, NPAIR + j), ("nodes", 2): (normed, 3 * NPAIR + j),
                  ("nodes", 3): (pre_ready, j)}
            signal, index = by[ph, stage]
            return signal.sem, signal.at(ph, i, index - back * signal.per[ph])

        block = ctx.enter_context(nc.Block())

        @block.sync
        def _(sp):
            full = (TILES - 1) * P
            sp.wait_ge(s_ms, 4)
            for n, name in enumerate(["src", "dst"]):
                sp.dma_start(edge_in[0:TILES - 1, n, :],
                             ins[name][0:full].rearrange("(t p) -> t p", p=P)).then_inc(s_ld, 16)
                sp.dma_start(edge_in[TILES - 1:TILES, n, 0:EDGES - full],
                             ins[name][full:EDGES].rearrange("(a p) -> a p", a=1)).then_inc(s_ld, 16)
            sp.dma_start(ew_in[0:TILES - 1, :],
                         ins["edge_weight"][0:full].rearrange("(t p) -> t p", p=P)).then_inc(s_ld, 16)
            sp.dma_start(ew_in[TILES - 1:TILES, 0:EDGES - full],
                         ins["edge_weight"][full:EDGES].rearrange("(a p) -> a p", a=1)).then_inc(s_ld, 16)
            for n, name in enumerate(["L1_gnn_W", "L1_gnn_W1", "L3_gnn_W0", "L3_gnn_W1"]):
                sp.dma_start(w_in[:, n, :, :],
                             ins[name].rearrange("(c p) n -> p c n", p=P)).then_inc(s_ld_w, 16)
            for name, to in (("L1_gnn_W2", W_head), ("L2_gnn_W", W_sum)):
                sp.dma_start(to[:, :, :], ins[name].rearrange("(c p) n -> p c n", p=P)).then_inc(s_ld_w, 16)
            for n, name in enumerate(["L1_gnn_b", "L1_gnn_b1", "L3_gnn_g0", "L3_gnn_beta0"]):
                for c in range(2):
                    sp.dma_start(b_cols[:, c, n:n + 1], ins[name][c * P:(c + 1) * P]
                                 .rearrange("(p a) -> p a", a=1)).then_inc(s_ld_w, 16)
            for n, name in enumerate(["L1_gnn_b2", "L3_gnn_b0", "L3_gnn_b1"]):
                for k in range(3):
                    sp.dma_start(b_three[32 * k:32 * k + 1, n, :],
                                 ins[name].rearrange("(a n) -> a n", a=1)).then_inc(s_ld_w, 16)
            for name, to in (("L2_gnn_b", b_sum), ("L3_gnn_g1", g_last), ("L3_gnn_beta1", beta_last)):
                sp.dma_start(to[:, :], ins[name].rearrange("(a n) -> a n", a=1)
                             .to_broadcast([P, D])).then_inc(s_ld_w, 16)

            sp.wait_ge(s_dve, DVE_NODE_REC)
            sp.dma_start(node_tab.rearrange("(c p l) f -> p c (l f)", c=2, p=P),
                         node_rec[:, :, :, :].rearrange("p c l f -> p c (l f)")).then_inc(node_stored, 16)

            sp.wait_ge(s_dve, DVE_NONE_ROW)
            sp.dma_start(table[NONE:NONE + 1, :], none_row[:, :]).then_inc(table_stored[0].sem, 16)
            for k in range(3):
                sp.dma_start(column[k][NONE:NONE + 1, :],
                             none_row[:, k * D:(k + 1) * D]).then_inc(column_stored[0].sem, 16)
            for n, s in enumerate((*resid_stored, table_stored[1], column_stored[1], out_stored)):
                sp.dma_start(scratch["begin"][n:n + 1, :], none_row[:, 0:D]).then_inc(s.sem, 16)
            for h in range(2):
                sp.wait_ge(rec_scattered[h], 16 * (TILES // 2))
            def load_rec(ph, i):
                sp.dma_start(rec_land[:, :].rearrange("p (t f) -> p t f", f=RF),
                             rec_sorted[bass.ds(i * (EG * P), EG * P), :]
                             .rearrange("(t p) f -> p t f", p=P)).then_inc(rec_loaded.sem, 16)

            def load_state(ph, i, h):
                a, b = HALVES[h]
                sp.dma_start(rows[:, a:b, :], state[bass.ds(i, 1), :, a:b, :]
                             .rearrange("a p t f -> (a p) t f")).then_inc(rows_loaded[h].sem, 16)

            def store_state(ph, i, h):
                a, b = HALVES[h]
                sp.dma_start(state[bass.ds(i, 1), :, a:b, :].rearrange("a p t f -> (a p) t f"),
                             resid[:, a:b, :]).then_inc(resid_stored[h].sem, 16)

            def store_table(ph, i, h):
                a, b = HALVES[h]
                k = int(ph[-1]) - 1
                if ph == "edges2":
                    sp.wait_ge(leaky_ready.sem, leaky_ready.at(ph, i, b // 2 - 1))
                else:
                    sp.wait_ge(sums_copied.sem, sums_copied.at(ph, i, b - 1))
                what = pre if ph == "edges2" else sums
                at = bass.ds(i * (EG * P) + a * P, (b - a) * P)
                if k < 3:
                    sp.dma_start(column[k][at, :].rearrange("(t p) f -> p t f", p=P),
                                 what[:, a:b, :]).then_inc(column_stored[h].sem, 16)
                sp.dma_start(table[at, k * D:(k + 1) * D].rearrange("(t p) f -> p t f", p=P),
                             what[:, a:b, :]).then_inc(table_stored[h].sem, 16)

            def edges_pass(ph, i, before, more):
                if more:
                    sp.wait_ge(work_ready.sem, work_ready.at(ph, i, 0))
                    for h, (a, b) in enumerate(HALVES):
                        sp.wait_ge(gathered[h].sem, gathered[h].at(ph, i, b - a - 1))
                    load_rec(ph, i + 1)
                for h in range(2):
                    if before:
                        store_table(ph, i - 1, h)
                    if ph != "edges4":
                        sp.wait_ge(resid_ready.sem, resid_ready.at(ph, i, HALVES[h][1] // 2 - 1))
                        store_state(ph, i, h)
                    else:
                        sp.wait_ge(normed.sem, normed.at(ph, i, HALVES[h][1] // 2 - 1))
                    if more and ph != "edges1":
                        load_state(ph, i + 1, h)

            def load_first(ph, before):
                for h in range(2):
                    sp.wait_ge(gathered[h].sem, gathered[h].all(before))
                sp.wait_ge(work_ready.sem, work_ready.all(before))
                load_rec(ph, 0)

            load_rec("edges1", 0)
            for n, (ph, passes) in enumerate(PHASES[:-1]):
                edges_pass(ph, 0, False, True)
                with sp.Fori(1, passes - 1) as i:
                    edges_pass(ph, i, True, True)
                edges_pass(ph, passes - 1, True, False)
                after = PHASES[n + 1][0]
                if after != "nodes":
                    load_first(after, ph)
                    store_table(ph, passes - 1, 0)
                    for h in range(2):
                        sp.wait_ge(resid_stored[h].sem, resid_stored[h].all(ph))
                        load_state(after, 0, h)
                    store_table(ph, passes - 1, 1)

            ph = "nodes"

            def load_nodes(row):
                sp.dma_start(node_land[:, :], node_tab[bass.ds(row, NROWS), :]
                             .rearrange("(p t) f -> p (t f)", p=P)).then_inc(rec_loaded.sem, 16)

            def load_rows(row):
                sp.dma_start(rows[:, 0:NG, :], x[bass.ds(row, NROWS), :]
                             .rearrange("(p t) f -> p t f", p=P)).then_inc(rows_loaded[0].sem, 16)

            def next_nodes(i, row):
                sp.wait_ge(work_ready.sem, work_ready.at(ph, i, 0))
                sp.wait_ge(gathered[0].sem, gathered[0].at(ph, i, NG - 1))
                load_nodes(row)
                sp.wait_ge(resid_ready.sem, resid_ready.at(ph, i, NPAIR - 1))
                load_rows(row)

            def store_nodes(i, row):
                sp.wait_ge(out_ready.sem, out_ready.at(ph, i, NPAIR - 1))
                sp.dma_start(out[bass.ds(row, NROWS), :].rearrange("(p t) f -> p t f", p=P),
                             pre[:, 0:NG, :]).then_inc(out_stored.sem, 16)

            sp.wait_ge(normed.sem, normed.all("edges4"))
            for h in range(2):
                sp.wait_ge(gathered[h].sem, gathered[h].all("edges4"))
            sp.wait_ge(work_ready.sem, work_ready.all("edges4"))
            load_nodes(0)
            load_rows(0)
            for h in range(2):
                store_table("edges4", EGROUPS - 1, h)
            next_nodes(0, NROWS)
            with sp.Fori(1, NGROUPS - 2) as i:
                next_nodes(i, i * NROWS + NROWS)
                store_nodes(i - 1, i * NROWS - NROWS)
            next_nodes(NGROUPS - 2, LAST)
            store_nodes(NGROUPS - 3, (NGROUPS - 3) * NROWS)
            store_nodes(NGROUPS - 2, (NGROUPS - 2) * NROWS)
            sp.wait_ge(out_stored.sem, out_stored.at(ph, NGROUPS - 2, 0))
            store_nodes(NGROUPS - 1, LAST)
            sp.wait_ge(out_stored.sem, out_stored.all(ph))
            for h in range(2):
                sp.wait_ge(table_stored[h].sem, table_stored[h].all("edges4"))
                sp.wait_ge(column_stored[h].sem, column_stored[h].all("edges3"))
                sp.wait_ge(resid_stored[h].sem, resid_stored[h].all("edges3"))

        @block.gpsimd
        def _(pool):
            for s in primed:
                pool.sem_inc(s.sem, PRIME)
            nc.gpsimd.memset(ident[:, :], 0.0).then_inc(s_pool, 1)
            nc.gpsimd.memset(earlier[:, :], 1.0).then_inc(s_pool, 1)
            nc.gpsimd.memset(later[:, :], 1.0).then_inc(s_pool, 1)
            nc.gpsimd.memset(is_last[:, :], 0.0).then_inc(s_pool, 1)
            pool.wait_ge(s_pool, 4)
            nc.gpsimd.affine_select(out=ident[:, :], in_=ident[:, :], compare_op=ALU.not_equal, fill=1.0,
                                    base=0, pattern=[[-1, P]], channel_multiplier=1).then_inc(s_cst, 1)
            nc.gpsimd.affine_select(out=earlier[:, :], in_=earlier[:, :], compare_op=ALU.is_gt, fill=0.0,
                                    base=0, pattern=[[-1, P]], channel_multiplier=1).then_inc(s_cst, 1)
            nc.gpsimd.affine_select(out=later[:, :], in_=later[:, :], compare_op=ALU.is_gt, fill=0.0,
                                    base=0, pattern=[[1, P]], channel_multiplier=-1).then_inc(s_cst, 1)
            nc.gpsimd.affine_select(out=is_last[:, :], in_=is_last[:, :], compare_op=ALU.not_equal, fill=1.0,
                                    base=-(P - 1), pattern=[[0, 1]], channel_multiplier=1).then_inc(s_cst, 1)
            nc.gpsimd.iota(count_f[:, :], [[1, LO]], base=0, channel_multiplier=0,
                           allow_small_or_imprecise_dtypes=True).then_inc(s_cst, 1)
            nc.gpsimd.iota(part[:, :], [[P, 2]], base=0, channel_multiplier=1,
                           allow_small_or_imprecise_dtypes=True).then_inc(s_cst, 1)

            pool.wait_ge(s_dve, DVE_READY)
            with pool.Fori(0, TILES // 2) as i:
                for q in range(2):
                    pool.wait_ge(oh_lo_ready, i * 2 + q + 1)
                    nc.gpsimd.tensor_tensor(oh_lo_w[:, q, :, :], oh_lo[:, q:q + 1, :].to_broadcast([P, 3, LO]),
                                            ew_part[:, :, bass.ds(i * 2 + q, 1)].to_broadcast([P, 3, LO]),
                                            ALU.mult).then_inc(lo_weighted, 1)

            def gather_ends(i, h):
                pool.wait_ge(idx_ready[h], i * 2 + 2)
                pool.sem_inc(pool_past, 1)
                for g in range(BG):
                    for n, to in ((0, ns[h]), (1, nd[h])):
                        nc.gpsimd.indirect_dma_start(
                            to[:, g, :], None, node_tab,
                            bass.IndirectOffsetOnAxis(ap=idx2[h][:, n, g:g + 1], axis=0),
                            bounds_check=HI * LO - 1).then_inc(ends_gathered[h], 16)

            def scatter_records(i, h):
                pool.wait_ge(rec_ready[h], i + 1)
                pool.sem_inc(pool_past, 1)
                for g in range(BG):
                    nc.gpsimd.indirect_dma_start(
                        rec_sorted, bass.IndirectOffsetOnAxis(ap=rec_at[h][:, g:g + 1], axis=0),
                        rec[h][:, g, :], None, bounds_check=TILES * P - 1).then_inc(rec_scattered[h], 16)

            pool.wait_ge(node_stored, 16)
            gather_ends(0, 0)
            with pool.Fori(0, BGROUPS // 2 - 1) as i:
                gather_ends(i, 1)
                scatter_records(i, 0)
                gather_ends(i + 1, 0)
                scatter_records(i, 1)
            gather_ends(BGROUPS // 2 - 1, 1)
            scatter_records(BGROUPS // 2 - 1, 0)
            scatter_records(BGROUPS // 2 - 1, 1)

            def power(ph, i, n, own=None):
                a = 2 * (n % pairs(ph))
                b = a + 2
                pool.wait_ge(moments_ready.sem, moments_ready.at(ph, i, n))
                nc.gpsimd.tensor_tensor(var_eps[:, a:b], moments[:, a:b, 1], eps_w[:, a:b],
                                        ALU.add).then_inc(eps_added.sem, 1)
                pool.wait_ge(eps_added.sem, eps_added.at(ph, i, n))
                if own is None:
                    nc.gpsimd.tensor_tensor(rstd[:, a:b], var_eps[:, a:b], minus_half[:, a:b],
                                            ALU.pow).then_inc(rstd_ready.sem, 1)
                else:
                    nc.gpsimd.tensor_tensor(rstd[:, a:b], var_eps[:, a:b], minus_half[:, a:b],
                                            ALU.pow).then_inc(rstd_raw.sem, 1)
                    pool.wait_ge(rstd_raw.sem, rstd_raw.at(ph, i, n % pairs(ph)))
                    nc.gpsimd.tensor_tensor(rstd[:, a:b], rstd[:, a:b], own[:, a:b],
                                            ALU.mult).then_inc(rstd_ready.sem, 1)

            def gather_edges(ph, src, field, j):
                pool.sem_inc(pool_past, 1)
                for g in (2 * j, 2 * j + 1):
                    nc.gpsimd.indirect_dma_start(
                        rows[:, g, :] if ph == "edges1" else got_e[:, g, :], None, src,
                        bass.IndirectOffsetOnAxis(
                            ap=rec_land[:, g * RF + field:g * RF + field + 1].bitcast(I32), axis=0),
                        bounds_check=src.shape[0] - 1).then_inc(gathered[g // HALF].sem, 16)

            def edges_pass(ph, src, field, i, more):
                for n in range(steps(ph)):
                    if ph == "edges2" and n < EP:
                        if n == 0:
                            pool.wait_ge(work_ready.sem, work_ready.at(ph, i, 0))
                        power(ph, i, n, rec_now[:, :, R_SELF])
                    else:
                        power(ph, i, n)
                    if more and n >= steps(ph) - EP:
                        j = n - (steps(ph) - EP)
                        if j == 0:
                            pool.wait_ge(rec_loaded.sem, rec_loaded.at(ph, i + 1, 0))
                        if ph in ("edges1", "edges3"):
                            pool.wait_ge(resid_ready.sem, resid_ready.at(ph, i, j))
                        else:
                            pool.wait_ge(plus_ready.sem, plus_ready.at(ph, i, j))
                        gather_edges(ph, src, field, j)

            for ph, field, src in (("edges1", R_DST, x), ("edges2", R_LAST, column[0]),
                                   ("edges3", R_LAST, column[1]), ("edges4", R_LAST, column[2])):
                if ph != "edges1":
                    before = f"edges{int(ph[-1]) - 1}"
                    for h in range(2):
                        pool.wait_ge(column_stored[h].sem, column_stored[h].all(before))
                    pool.wait_ge(plus_ready.sem, plus_ready.all(before))
                    pool.wait_ge(resid_ready.sem, resid_ready.all(before))
                pool.wait_ge(rec_loaded.sem, rec_loaded.at(ph, 0, 0))
                for j in range(EP):
                    gather_edges(ph, src, field, j)
                with pool.Fori(0, EGROUPS - 1) as i:
                    edges_pass(ph, src, field, i, True)
                edges_pass(ph, src, field, EGROUPS - 1, False)

            ph = "nodes"

            def gather_nodes(j):
                pool.sem_inc(pool_past, 1)
                for g in (2 * j, 2 * j + 1):
                    nc.gpsimd.indirect_dma_start(
                        got[:, g, :], None, table,
                        bass.IndirectOffsetOnAxis(
                            ap=node_land[:, g * NF + N_LAST:g * NF + N_LAST + 1].bitcast(I32), axis=0),
                        bounds_check=NONE).then_inc(gathered[0].sem, 16)

            def nodes_slot(i, n, main, before):
                s, j = divmod(n, NPAIR)
                if main:
                    if s == 1:
                        if j == 0:
                            pool.wait_ge(work_ready.sem, work_ready.at(ph, i, 0))
                        power(ph, i, n, node_now[:, :, N_DINV2])
                    else:
                        power(ph, i, n)
                m = pair_at(n, 1)
                if before and m is not None:
                    a, b = 2 * m, 2 * m + 2
                    pool.wait_ge(moments_ready_l.sem, moments_ready_l.at(ph, i, m - NPAIR))
                    nc.gpsimd.tensor_tensor(var_eps_l[:, a:b], moments_l[:, a:b, 1], eps_w[:, a:b],
                                            ALU.add).then_inc(eps_added_l.sem, 1)
                    pool.wait_ge(eps_added_l.sem, eps_added_l.at(ph, i, m - NPAIR))
                    nc.gpsimd.tensor_tensor(rstd_l[:, a:b], var_eps_l[:, a:b], minus_half[:, a:b],
                                            ALU.pow).then_inc(rstd_ready_l.sem, 1)
                if main and before and s == 0:
                    pool.wait_ge(pre_ready.sem, pre_ready.at(ph, i, j - NPAIR))
                    if j == 0:
                        pool.wait_ge(rec_loaded.sem, rec_loaded.at(ph, i, 0))
                    gather_nodes(j)
                if main and not before and n == NPAIR - 1:
                    for h in range(2):
                        pool.wait_ge(table_stored[h].sem, table_stored[h].all("edges4"))
                        pool.wait_ge(column_stored[h].sem, column_stored[h].all("edges4"))
                    pool.wait_ge(plus_ready.sem, plus_ready.all("edges4"))
                    pool.wait_ge(rec_loaded.sem, rec_loaded.at(ph, i, 0))
                    for m in range(NPAIR):
                        gather_nodes(m)
                if main and s == 1:
                    if j == 0:
                        pool.wait_ge(gathered[0].sem, gathered[0].at(ph, i, NG - 1))
                    pool.wait_ge(resid_ready.sem, resid_ready.at(ph, i, j))
                    nc.gpsimd.tensor_tensor(skip[:, 2 * j:2 * j + 2, :], resid[:, 2 * j:2 * j + 2, :],
                                            got[:, 2 * j:2 * j + 2, D:2 * D],
                                            ALU.add).then_inc(skip_ready.sem, 1)

            for n in range(SLOTS):
                nodes_slot(0, n, True, False)
            with pool.Fori(1, NGROUPS) as i:
                for n in range(SLOTS):
                    nodes_slot(i, n, True, True)
            for n in range(SLOTS):
                nodes_slot(NGROUPS, n, False, True)

        @block.scalar
        def _(act):
            act.wait_ge(s_dve, DVE_READY)

            def pick(t, q):
                nc.scalar.copy(spread_now[:, q, :], to_spread[:, bass.ds(t, 1), :].rearrange("p a n -> p (a n)")
                               ).then_inc(cols_picked, 1)

            def one_edge_tile(t, q, more):
                if more:
                    act.wait_ge(spread_done, t + 1)
                    pick(t + 2, q)
                act.wait_ge(oh_dst_ready, t + 1)
                for k in range(3):
                    done = nc.scalar.activation(oh_dst_w[:, q, k, :], oh_dst[:, q, :], ACT.Copy,
                                                scale=ew_part[:, k, bass.ds(t, 1)])
                done.then_inc(hot_ready, 1)
                act.wait_ge(pairs_done, t + 1)
                act.wait_ge(mask_updated, t + 2)
                nc.scalar.copy(hits[:, :], bank[5][:, :]).then_inc(hits_copied, 1)
                act.wait_ge(hist_done, t + 1)
                nc.scalar.copy(counts[:, :, :].rearrange("p c l -> p (c l)"), bank[6][:, :]).then_inc(hist_copied, 1)

            pick(0, 0)
            pick(1, 1)
            with act.Fori(0, TILES // 2 - 1) as i:
                for q in range(2):
                    one_edge_tile(i * 2 + q, q, True)
            one_edge_tile(TILES - 2, 0, False)
            one_edge_tile(TILES - 1, 1, False)
            act.wait_ge(s_dve, DVE_ROOT1)
            nc.scalar.activation(tmp[:, 2, :, :], tmp[:, 0, :, :], ACT.Sqrt).then_inc(s_roots, 1)
            act.wait_ge(s_dve, DVE_ROOT2)
            nc.scalar.activation(tmp[:, 0, :, :], tmp[:, 3, :, :], ACT.Sqrt).then_inc(s_roots, 1)

            def evacuate(ph, i, n, func):
                a = 2 * (n % pairs(ph))
                ring = turn_ring(ph)
                act.wait_ge(turn_done.sem, turn_done.at(ph, i, n))
                nc.scalar.activation(turned[:, a:a + 2, :], ring[n % len(ring)][:, :]
                                     .rearrange("p (t f) -> p t f", f=D), func).then_inc(turned_ready.sem, 1)

            def evacuate_silu(ph, i, n):
                a = 2 * (n % pairs(ph))
                ring = turn_ring(ph)
                act.wait_ge(turn_done.sem, turn_done.at(ph, i, n))
                for c in range(2):
                    done = nc.scalar.activation(
                        turned[:, a:a + 2, c * P:(c + 1) * P],
                        ring[n % len(ring)][:, :].rearrange("p (t f) -> p t f", f=D)[:, :, c * P:(c + 1) * P],
                        ACT.Silu, bias=b_cols[:, c, 3:4], scale=b_cols[:, c, 2:3])
                done.then_inc(turned_ready.sem, 1)

            def hide(ph, i, n):
                j = n % pairs(ph)
                ring = prod_ring(ph)
                act.wait_ge(hidden_done.sem, hidden_done.at(ph, i, j))
                for c in range(2):
                    done = nc.scalar.activation(
                        hidden[:, c, 2 * j:2 * j + 2, :], ring[n % len(ring)][:, c * D:c * D + D]
                        .rearrange("p (t r) -> p t r", r=P), ACT.Relu, bias=b_gcn[:, c:c + 1])
                done.then_inc(hidden_ready.sem, 1)

            def copy_sums(ph, i, g):
                if ph == "edges2":
                    act.wait_ge(leaky_ready.sem, leaky_ready.at(ph, i, g // 2 - EP))
                else:
                    h = g // HALF
                    act.wait_ge(table_stored[h].sem, table_stored[h].at(ph, i, -1))
                    act.wait_ge(column_stored[h].sem, column_stored[h].at(ph, i, -1))
                act.wait_ge(summed.sem, summed.at(ph, i, g))
                nc.scalar.copy(sums[:, g, :], sum_bank[g % 2][:, 0:D]).then_inc(sums_copied.sem, 1)

            def act_slot(ph, i, n):
                stage = n // pairs(ph)
                if n < TURNED[ph] * pairs(ph):
                    if (ph, stage) in (("edges1", 0), ("edges2", 1), ("nodes", 0)):
                        evacuate(ph, i, n, ACT.Relu)
                    elif (ph, stage) in (("edges4", 1), ("nodes", 3)):
                        evacuate_silu(ph, i, n)
                    else:
                        evacuate(ph, i, n, ACT.Copy)
                if n >= 1 and HIDDEN.get(ph) == (n - 1) // pairs(ph):
                    hide(ph, i, n - 1)

            def nodes_slot(i, n, main, before):
                m = pair_at(n, 3)
                if before and m is not None:
                    act.wait_ge(shifted.sem, shifted.at("nodes", i, m - NPAIR))
                    nc.scalar.activation(pre[:, 2 * m:2 * m + 2, :], pre[:, 2 * m:2 * m + 2, :],
                                         ACT.Silu).then_inc(silu_ready.sem, 1)
                if main:
                    act_slot("nodes", i, n)

            def edges_pass(ph, i, main, before):
                for n in range(steps(ph) + (TURNED[ph] == MEASURED[ph])):
                    for k, j in adding(ph, i, n, main, before):
                        copy_sums(ph, k, 2 * j)
                    if main:
                        act_slot(ph, i, n)
                    for k, j in adding(ph, i, n, main, before):
                        copy_sums(ph, k, 2 * j + 1)

            for ph, passes in PHASES[:-1]:
                edges_pass(ph, 0, True, False)
                with act.Fori(1, passes) as i:
                    edges_pass(ph, i, True, True)
                edges_pass(ph, passes, False, True)
            for n in range(SLOTS):
                nodes_slot(0, n, True, False)
            with act.Fori(1, NGROUPS) as i:
                for n in range(SLOTS):
                    nodes_slot(i, n, True, True)
            for n in range(SLOTS):
                nodes_slot(NGROUPS, n, False, True)

        @block.tensor
        def _(pe):
            def turn(to, what, n=P, start=True):
                return nc.tensor.transpose(to, what, ident[0:n, 0:n])

            pe.wait_ge(s_cst, 6)
            pe.wait_ge(s_dve, DVE_EDGE_F)
            for n in range(4):
                turn(bank[0][:, n * TILES:(n + 1) * TILES], edge_f[:, n, :], TILES)
            turn(bank[0][:, 4 * TILES:5 * TILES], ew_in[:, :], TILES).then_inc(s_pe, 1)
            pe.wait_ge(s_dve, DVE_ZEROS)
            pe.matmul(bank[6][:, :], zeros_b[:, 0:P], zeros_b[:, :], start=True, stop=True)
            pe.matmul(bank[7][:, :], zeros_b[:, 0:P], zeros_b[:, :], start=True, stop=True).then_inc(s_pe, 1)
            pe.wait_ge(s_dve, DVE_READY)

            def spread(t, q):
                pe.wait_ge(turn_hot_ready, t + 1)
                pe.wait_ge(cols_picked, t + 1)
                for n in range(3):
                    last = turn(bank[q][:, n * P:(n + 1) * P], spread_now[:, q, n:n + 1].to_broadcast([P, P]))
                last.then_inc(spread_done, 1)

            def one_edge_tile(t, q, more):
                pe.wait_ge(turn_hot_ready, t + 3)
                pe.wait_ge(hist_copied, t + 1)
                for c in range(2):
                    last = pe.matmul(bank[2 + q][:, 0:LO], oh_turn[:, q, c, :], counts[:, c, :],
                                     start=(c == 0), stop=(c == 1))
                last.then_inc(look_done, 1)
                pe.wait_ge(oh_dst_ready, t + 1)
                pe.wait_ge(mask_updated, t + 2)
                for c in range(2):
                    last = pe.matmul(bank[5][:, c * D:(c + 1) * D], oh_lo[:, q, c * P:(c + 1) * P],
                                     oh_dst[:, q, :], start=True, stop=True)
                last.then_inc(pairs_done, 1)
                pe.wait_ge(lo_weighted, t + 1)
                for c in range(2):
                    pe.matmul(bank[6][:, c * LO:(c + 1) * LO], oh_hi[:, q, c * P:(c + 1) * P],
                              oh_lo[:, q, :], start=False, stop=True, skip_group_check=True)
                    for k in range(3):
                        last = pe.matmul(bank[7][:, c * LO:(c + 1) * LO], oh_hi[:, q, c * P:(c + 1) * P],
                                         oh_lo_w[:, q, k, :], start=False, stop=True, skip_group_check=True)
                last.then_inc(hist_done, 1)
                if more:
                    spread(t + 2, q)
                pe.wait_ge(hot_ready, t + 1)
                for c in range(2):
                    for k in range(3):
                        last = pe.matmul(bank[4][:, c * D:(c + 1) * D], oh_lo[:, q, c * P:(c + 1) * P],
                                         oh_dst_w[:, q, k, :], start=(k == 0), stop=(k == 2))
                last.then_inc(weights_done, 1)

            spread(0, 0)
            spread(1, 1)
            with pe.Fori(0, TILES // 2 - 1) as i:
                for q in range(2):
                    one_edge_tile(i * 2 + q, q, True)
            one_edge_tile(TILES - 2, 0, False)
            one_edge_tile(TILES - 1, 1, False)
            pe.wait_ge(s_dve, DVE_SCAN)
            pe.matmul(bank[0][:, 0:2], later[:, :], scan[:, :, LO - 1], start=True, stop=True)
            pe.matmul(bank[1][:, 0:1], ones[:, :], scan[:, 0, LO - 1:LO], start=True, stop=True).then_inc(s_pe, 1)
            pe.wait_ge(s_ld_w, 16 * WEIGHT_LOADS)
            pe.wait_ge(s_dve, DVE_NODE_REC)
            for n, b in ((0, 1), (2, 2), (3, 3)):
                for c in range(2):
                    for r in range(2):
                        last = turn(bank[b][:, c * D + r * P:c * D + (r + 1) * P],
                                    w_in[:, n, r, c * P:(c + 1) * P])
            last.then_inc(s_pe, 1)
            pe.wait_ge(s_dve, DVE_W_TURN)
            for c in range(2):
                for k in range(2):
                    pe.matmul(bank[4][:, c * D:(c + 1) * D], w_turn[:, k, c * P:(c + 1) * P],
                              w_in[:, 1, k, :], start=(k == 0), stop=(k == 1))
            for c in range(2):
                for k in range(2):
                    last = pe.matmul(bank[5][:, c:c + 1], w_in[:, 1, k, c * P:(c + 1) * P],
                                     b_cols[:, k, 0:1], start=(k == 0), stop=(k == 1))
            last.then_inc(s_pe, 1)

            def turn_pair(ph, i, n):
                ring = turn_ring(ph)
                pe.wait_ge(*rows_to_turn(ph, i, n))
                pe.wait_ge(turned_ready.sem, turned_ready.at(ph, i, n - len(ring) if n >= len(ring) else -1))
                for t in range(2):
                    for c in range(2):
                        o = t * D + c * P
                        last = turn(ring[n % len(ring)][:, o:o + P],
                                    left[:, 2 * (n % pairs(ph)) + t, c * P:(c + 1) * P])
                last.then_inc(turn_done.sem, 1)

            def spread_sources(ph, i, q):
                if q == 0:
                    pe.wait_ge(work_ready.sem, work_ready.at(ph, i, 0))
                pe.wait_ge(same_ready.sem, same_ready.at(ph, i, 2 * q - 1))
                for g in range(4 * q, min(4 * q + 4, EG)):
                    last = turn(spread_bank[:, g % 4 * P:g % 4 * P + P],
                                rec_now[:, g, R_SRC:R_SRC + 1].to_broadcast([P, P]))
                last.then_inc(src_spread.sem, 1)

            def bank_free(ph, i, n):
                ring, steps = len(prod_ring(ph)), TURNED[ph] * pairs(ph)
                k = n % steps
                back = 1 if n < 0 else 0
                if k >= ring:
                    k -= ring
                else:
                    back += 1
                    k = max(m for m in range(steps) if m % ring == k)
                pe.wait_ge(*product_read(ph, i, k, back))

            def multiply(ph, i, n, weight, bias=None):
                k = n % (TURNED[ph] * pairs(ph))
                ring = prod_ring(ph)
                bank_ = ring[k % len(ring)]
                pe.wait_ge(turned_ready.sem, turned_ready.at(ph, i, n))
                bank_free(ph, i, n)
                for t in range(2):
                    o = bank_[:, t * D:t * D + D]
                    for c in range(2):
                        last = pe.matmul(o, turned[:, 2 * (k % pairs(ph)) + t, c * P:(c + 1) * P],
                                         weight[:, c, :], start=(c == 0), stop=(c == 1 and bias is None))
                    if bias is not None:
                        last = pe.matmul(o, ones_b[:, :], b_rows[:, bias, :], start=False, stop=True)
                last.then_inc(product.sem, 1)

            def multiply_hidden(ph, i, n):
                a = 2 * (n % pairs(ph))
                ring = prod_ring(ph)
                pe.wait_ge(turned_ready.sem, turned_ready.at(ph, i, n))
                bank_free(ph, i, n)
                for m in range(2):
                    for c in range(2):
                        last = pe.matmul(ring[n % len(ring)][:, m * D:m * D + D]
                                         .rearrange("p (t r) -> p t r", r=P),
                                         W_gcn[:, c, m * P:(m + 1) * P],
                                         turned[:, a:a + 2, c * P:(c + 1) * P],
                                         start=(c == 0), stop=(c == 1))
                last.then_inc(hidden_done.sem, 1)

            def multiply_head(ph, i, n):
                j = n % pairs(ph)
                ring = prod_ring(ph)
                pe.wait_ge(hidden_ready.sem, hidden_ready.at(ph, i, j))
                for t in range(2):
                    o = ring[n % len(ring)][:, t * D:t * D + D]
                    for c in range(2):
                        pe.matmul(o, hidden[:, c, 2 * j + t, :], W_head[:, c, :], start=(c == 0), stop=False)
                    last = pe.matmul(o, ones_b[:, :], b_rows[:, 0, :], start=False, stop=True)
                last.then_inc(product.sem, 1)

            def add_within(ph, i, g):
                pe.wait_ge(message_ready.sem, message_ready.at(ph, i, g // 2))
                pe.wait_ge(same_ready.sem, same_ready.at(ph, i, g // 2))
                pe.wait_ge(sums_copied.sem, sums_copied.at(ph, i, g - 2))
                pe.matmul(sum_bank[g % 2][:, 0:D], same[:, g, :], message(g), start=True, stop=False)

            def add_carried(ph, i, g):
                pe.wait_ge(sums_copied.sem, sums_copied.at(ph, i, g - 1))
                pe.matmul(sum_bank[g % 2][:, 0:D], goes_on[:, g, :], sums[:, (g - 1) % EG, :],
                          start=False, stop=True).then_inc(summed.sem, 1)

            WEIGHTS = {"edges1": [(W_mask, None)], "edges2": [None, (W_sum, None)], "edges3": [],
                       "edges4": [(W_av0, 1), (W_av1, None)],
                       "nodes": [(W_mask, None), None, (W_av0, 1), (W_av1, 2)]}
            def product_of(ph, i, n):
                weight = WEIGHTS[ph][(n // pairs(ph)) % len(WEIGHTS[ph])]
                if weight is None:
                    multiply_hidden(ph, i, n)
                else:
                    multiply(ph, i, n, *weight)

            def pe_slot(ph, i, n, before):
                if n < TURNED[ph] * pairs(ph):
                    turn_pair(ph, i, n)
                head = n >= 2 and HIDDEN.get(ph) == (n - 2) // pairs(ph)
                head_last = head and HIDDEN[ph] == (n - 1) // pairs(ph)
                if head and not head_last:
                    multiply_head(ph, i, n - 2)
                if 1 <= n <= TURNED[ph] * pairs(ph) or before:
                    product_of(ph, i, n - 1)
                if head_last:
                    multiply_head(ph, i, n - 2)

            def edges_pass(ph, i, main, before):
                for n in range(steps(ph)):
                    for q in range((EP + 1) // 2):
                        if main and spread_slot(ph, q) == n:
                            spread_sources(ph, i, q)
                    for k, j in adding(ph, i, n, main, before):
                        add_within(ph, k, 2 * j)
                        add_carried(ph, k, 2 * j)
                        add_within(ph, k, 2 * j + 1)
                    if main:
                        pe_slot(ph, i, n, False)
                    for k, j in adding(ph, i, n, main, before):
                        add_carried(ph, k, 2 * j + 1)
                if main and TURNED[ph] * EP == steps(ph):
                    pe_slot(ph, i, steps(ph), False)

            for ph, passes in PHASES[:-1]:
                edges_pass(ph, 0, True, False)
                with pe.Fori(1, passes) as i:
                    edges_pass(ph, i, True, True)
                edges_pass(ph, passes, False, True)
            pe.wait_ge(sums_copied.sem, sums_copied.all("edges4"))
            for n in range(SLOTS):
                pe_slot("nodes", 0, n, False)
            with pe.Fori(1, NGROUPS) as i:
                for n in range(SLOTS):
                    pe_slot("nodes", i, n, True)
            product_of("nodes", NGROUPS, -1)

        @block.vector
        def _(dve):
            v = nc.vector
            step = [0]

            def link(ins_):
                step[0] += 1
                ins_.then_inc(s_dve, 1)
                dve.wait_ge(s_dve, step[0])
                return step[0]

            v.memset(edge_in[:, 0, :], PAD_NODE).then_inc(s_ms, 1)
            v.memset(edge_in[:, 1, :], 0).then_inc(s_ms, 1)
            v.memset(ew_in[:, :], 0.0).then_inc(s_ms, 1)
            v.memset(b_three[:, :, :], 0.0).then_inc(s_ms, 1)
            v.memset(b_rows[:, :, :], 0.0)
            v.memset(ones_b[:, :], 1.0)
            v.memset(ones[:, :], 1.0)
            v.memset(ones_w[:, :], 1.0)
            v.memset(minus_half[:, :], -0.5)
            v.memset(eps_w[:, :], EPS)
            v.memset(sums[:, EG - 1, :], 0.0)
            v.memset(W_mask[:, :, :], 0.0)
            v.memset(counts[:, :, :], 0.0)
            v.memset(node_rec[:, :, :, :], 0.0)
            v.memset(rec[0][:, :, :], 0.0)
            v.memset(rec[1][:, :, :], 0.0)
            v.memset(none_row[:, :], 0.0)
            assert link(v.memset(zeros_b[:, :], 0.0)) == DVE_ZEROS
            dve.wait_ge(s_ms, 4)
            dve.wait_ge(s_ld, 16 * EDGE_LOADS)
            dve.wait_ge(s_cst, 6)
            link(v.tensor_scalar(edge_lohi[:, 0, :], edge_in[:, 0, :], LO - 1, None, ALU.bitwise_and))
            link(v.tensor_scalar(edge_lohi[:, 1, :], edge_in[:, 0, :], 8, None, ALU.logical_shift_right))
            link(v.tensor_copy(edge_f[:, 0:2, :], edge_in[:, 0:2, :]))
            assert link(v.tensor_copy(edge_f[:, 2:4, :], edge_lohi[:, :, :])) == DVE_EDGE_F
            v.tensor_copy(count_b[:, :], count_f[:, :])
            dve.wait_ge(s_pe, 1)
            link(v.tensor_copy(cols[:, :, :].rearrange("p n t -> p (n t)"), bank[0][:, 0:5 * TILES]))
            v.tensor_copy(cols_i[:, :, :], cols[:, 0:2, :])
            v.tensor_scalar(first_hi[:, :], cols[:, C_HI, :], 0.0, None, ALU.is_equal)
            link(v.tensor_scalar(dst_cut[:, :], cols[:, C_DST, :], float(LO), None, ALU.min))
            v.scalar_tensor_tensor(key[:, :], cols[:, C_SRC, :], float(LO + 1), dst_cut[:, :], ALU.mult, ALU.add)
            v.tensor_copy(to_spread[:, :, 0], cols[:, C_SRC, :])
            v.tensor_copy(to_spread[:, :, 2], cols[:, C_HI, :])
            link(v.tensor_copy(ew_b[:, 0, :], cols[:, C_EW, :]))
            v.tensor_copy(to_spread[:, :, 1], key[:, :])
            link(v.tensor_copy(ew_part[:, 0, :], ew_b[:, 0, :]))
            link(v.tensor_tensor(ew_rest[:, 0, :], cols[:, C_EW, :], ew_part[:, 0, :], ALU.subtract))
            link(v.tensor_copy(ew_b[:, 1, :], ew_rest[:, 0, :]))
            link(v.tensor_copy(ew_part[:, 1, :], ew_b[:, 1, :]))
            link(v.tensor_tensor(ew_rest[:, 1, :], ew_rest[:, 0, :], ew_part[:, 1, :], ALU.subtract))
            link(v.tensor_copy(ew_b[:, 2, :], ew_rest[:, 1, :]))
            link(v.tensor_copy(ew_part[:, 2, :], ew_b[:, 2, :]))
            assert step[0] == DVE_READY
            dve.wait_ge(s_pe, 2)
            dve.sem_inc(turn_hot_ready, 2)
            dve.sem_inc(hist_copied, 1)
            dve.sem_inc(mask_updated, 2)

            def column_of(array, t, n=None):
                return array[:, bass.ds(t, 1)] if n is None else array[:, n, bass.ds(t, 1)]

            def make_hot(t, q):
                dve.wait_ge(mask_updated, t + 1)
                v.tensor_scalar(oh_lo[:, q, :], count_b[:, :], column_of(cols, t, C_LO), None, ALU.is_equal)
                v.tensor_scalar(oh_hi[:, q, :], count_b[:, :], column_of(cols, t, C_HI), None,
                                ALU.is_equal).then_inc(oh_lo_ready, 1)
                dve.wait_ge(spread_done, t + 1)
                v.scalar_tensor_tensor(junk[:, q, 0, 0:P], bank[q][:, P:2 * P], column_of(key, t), later[:, :],
                                       ALU.is_equal, ALU.mult,
                                       accum_out=again[:, q:q + 1]).then_inc(dup_counted, 1)
                v.tensor_tensor(oh_turn[:, q, :, :],
                                bank[q][:, 2 * P:3 * P].rearrange("p (a n) -> p a n", a=1).to_broadcast([P, 2, P]),
                                part[:, :].rearrange("p (c a) -> p c a", a=1).to_broadcast([P, 2, P]), ALU.is_equal)
                v.scalar_tensor_tensor(junk[:, q, 0, P:2 * P], bank[q][:, 0:P], column_of(cols, t, C_SRC),
                                       earlier[:, :], ALU.is_equal, ALU.mult,
                                       accum_out=column_of(in_tile, t)).then_inc(turn_hot_ready, 1)
                dve.wait_ge(dup_counted, t + 1)
                v.tensor_scalar(keep[:, q:q + 1], again[:, q:q + 1], 0.0, column_of(first_hi, t),
                                ALU.is_equal, ALU.mult).then_inc(keep_ready, 1)
                dve.wait_ge(keep_ready, t + 1)
                v.tensor_scalar(oh_dst[:, q, :], count_b[:, :], column_of(cols, t, C_DST), keep[:, q:q + 1],
                                ALU.is_equal, ALU.mult).then_inc(oh_dst_ready, 1)

            def one_edge_tile(t, q, more):
                if more:
                    make_hot(t + 1, 1 - q)
                dve.wait_ge(look_done, t + 1)
                v.scalar_tensor_tensor(junk[:, q, 1, :], bank[2 + q][:, 0:LO], 1.0, oh_lo[:, q, :],
                                       ALU.mult, ALU.mult,
                                       accum_out=in_before[:, bass.ds(t, 1)])
                dve.wait_ge(weights_done, t + 1)
                dve.wait_ge(hits_copied, t + 1)
                dve.wait_ge(mask_updated, t + 2)
                dve.sem_inc(dve_past, 1)
                v.copy_predicated(W_mask[:, :, :].rearrange("p c n -> p (c n)"),
                                  hits[:, :].bitcast(U32), bank[4][:, :]).then_inc(mask_updated, 1)

            make_hot(0, 0)
            with dve.Fori(0, TILES // 2 - 1) as i:
                for q in range(2):
                    one_edge_tile(i * 2 + q, q, True)
            one_edge_tile(TILES - 2, 0, True)
            one_edge_tile(TILES - 1, 1, False)
            dve.wait_ge(mask_updated, TILES + 2)
            dve.wait_ge(hist_copied, TILES + 1)
            dve.wait_ge(hist_done, TILES)
            link(v.tensor_tensor(place[:, :], in_tile[:, :], in_before[:, :], ALU.add))
            for c in range(2):
                v.tensor_tensor_scan(scan[:, c, :], ones_w[:, :], counts[:, c, :], 0.0, ALU.mult, ALU.add)
            wdeg, ok, root, rest = (tmp[:, n, :, :] for n in range(4))
            link(v.tensor_scalar(wdeg, bank[7][:, :].rearrange("p (c l) -> p c l", c=2), 1.0, None, ALU.add))
            assert step[0] == DVE_SCAN
            link(v.tensor_scalar(ok, wdeg, 0.0, None, ALU.is_gt))
            link(v.tensor_scalar(wdeg, wdeg, 1e-30, None, ALU.max))


            def inverse_root(to, of, aside):
                link(v.reciprocal(to, to))
                link(v.scalar_tensor_tensor(aside, to, -0.5, to, ALU.mult, ALU.mult))
                link(v.tensor_tensor(aside, aside, of, ALU.mult))
                link(v.scalar_tensor_tensor(to, aside, 1.5, to, ALU.add, ALU.mult))

            dve.wait_ge(s_roots, 1)
            inverse_root(root, wdeg, rest)
            link(v.tensor_tensor(node_rec[:, :, :, N_DINV], root, ok, ALU.mult))
            v.tensor_tensor(node_rec[:, :, :, N_DINV2], node_rec[:, :, :, N_DINV],
                            node_rec[:, :, :, N_DINV], ALU.mult)
            dve.wait_ge(s_pe, 3)
            v.tensor_copy(base[:, 0:1], bank[0][:, 0:1])
            link(v.tensor_copy(base[:, 1:2], bank[0][:, 1:2]))
            link(v.tensor_tensor(base[:, 1:2], base[:, 1:2], bank[1][:, 0:1], ALU.add))
            for c in range(2):
                link(v.tensor_scalar(scan[:, c, :], scan[:, c, :], base[:, c:c + 1], None, ALU.add))
            link(v.tensor_tensor(node_rec[:, :, :, N_START], scan[:, :, :], counts[:, :, :], ALU.subtract))
            link(v.tensor_scalar(ok, counts[:, :, :], 0.0, None, ALU.is_gt))
            link(v.scalar_tensor_tensor(rest, scan[:, :, :], -1.0 - NONE, ok, ALU.add, ALU.mult))
            link(v.tensor_scalar(node_rec[:, :, :, N_LASTF], rest, float(NONE), None, ALU.add))
            v.tensor_copy(node_rec[:, :, :, N_LAST].bitcast(I32), node_rec[:, :, :, N_LASTF])
            link(v.tensor_scalar(rest, counts[:, :, :], 1.0, None, ALU.max))
            v.reciprocal(node_rec[:, :, :, N_MEAN], rest)
            dve.wait_ge(s_roots, 2)
            inverse_root(wdeg, rest, root)
            link(v.tensor_tensor(node_rec[:, :, :, N_WINV], wdeg, ok, ALU.mult))
            assert step[0] == DVE_NODE_REC

            def pick_ends(i, h):
                for n in range(2):
                    v.tensor_copy(idx2[h][:, n, :],
                                  cols_i[:, n, bass.ds(i * (2 * BG) + h * BG, BG)]).then_inc(idx_ready[h], 1)

            def make_records(i, h, first=False):
                at = bass.ds(i * (2 * BG) + h * BG, BG)
                to, s_, d_ = rec[h], ns[h], nd[h]
                if not first:
                    dve.wait_ge(rec_scattered[h], i * (16 * BG))
                dve.wait_ge(ends_gathered[h], i * (32 * BG) + 32 * BG)
                v.tensor_copy(to[:, :, R_SRC], cols[:, C_SRC, at])
                v.tensor_copy(to[:, :, R_DST].bitcast(I32), cols[:, C_DST, at])
                v.tensor_tensor(rec_at[h][:, :], s_[:, :, N_START], place[:, at], ALU.add)
                v.tensor_copy(to[:, :, R_LAST].bitcast(I32), d_[:, :, N_LASTF])
                v.tensor_tensor(to[:, :, R_C2], s_[:, :, N_WINV], d_[:, :, N_WINV], ALU.mult)
                v.tensor_copy(to[:, :, R_C3], s_[:, :, N_MEAN])
                v.tensor_copy(to[:, :, R_SELF], d_[:, :, N_DINV2])
                v.tensor_tensor(to[:, :, R_C1], s_[:, :, N_DINV], d_[:, :, N_DINV],
                                ALU.mult).then_inc(rec_step[h], 1)
                dve.wait_ge(rec_step[h], i + 1)
                v.tensor_tensor(to[:, :, R_C1], to[:, :, R_C1], cols[:, C_EW, at],
                                ALU.mult).then_inc(rec_ready[h], 1)

            pick_ends(0, 0)
            pick_ends(0, 1)

            dve.wait_ge(s_ld_w, 16 * WEIGHT_LOADS)
            dve.wait_ge(s_pe, 4)
            assert link(v.tensor_copy(w_turn[:, :, :].rearrange("p c n -> p (c n)"), bank[1][:, :])) == DVE_W_TURN
            v.tensor_copy(W_av0[:, :, :].rearrange("p c n -> p (c n)"), bank[2][:, :])
            v.tensor_copy(W_av1[:, :, :].rearrange("p c n -> p (c n)"), bank[3][:, :])
            link(v.tensor_copy(b_part[:, 0, :, :], b_three[:, :, :]))
            link(v.tensor_tensor(b_rest[:, :, :], b_three[:, :, :], b_part[:, 0, :, :], ALU.subtract))
            link(v.tensor_copy(b_part[:, 1, :, :], b_rest[:, :, :]))
            link(v.tensor_tensor(b_rest[:, :, :], b_rest[:, :, :], b_part[:, 1, :, :], ALU.subtract))
            link(v.tensor_copy(b_part[:, 2, :, :], b_rest[:, :, :]))
            for k in range(3):
                link(v.tensor_copy(b_rows[32 * k:32 * k + 1, :, :], b_part[32 * k:32 * k + 1, k, :, :]))
            dve.wait_ge(s_pe, 5)
            v.tensor_copy(W_gcn[:, :, :].rearrange("p c n -> p (c n)"), bank[4][:, :])
            v.tensor_tensor(b_gcn[:, :], bank[5][:, 0:2], b_cols[:, :, 1], ALU.add)
            link(v.scalar_tensor_tensor(none_row[:, D:2 * D], b_sum[0:1, :], ALPHA, b_sum[0:1, :],
                                        ALU.mult, ALU.max))
            assert step[0] == DVE_NONE_ROW

            for h in range(2):
                make_records(0, h, True)
                pick_ends(1, h)
            with dve.Fori(1, BGROUPS // 2 - 1) as i:
                for h in range(2):
                    make_records(i, h)
                    pick_ends(i + 1, h)
            for h in range(2):
                make_records(BGROUPS // 2 - 1, h)

            def source(ph, n):
                n %= MEASURED[ph] * pairs(ph)
                stage, j = divmod(n, pairs(ph))
                ring = prod_ring(ph)
                k = n - pairs(ph)
                for t in range(2):
                    g = 2 * j + t
                    if (ph, stage) in (("edges4", 1), ("nodes", 3)):
                        yield g, ring[k % len(ring)][:, t * D:t * D + D]
                    elif stage == 0 and ph != "edges3":
                        yield g, rows[:, g, :]
                    elif (ph, stage) == ("nodes", 2):
                        yield g, resid3[:, g, :]
                    else:
                        yield g, resid[:, g, :]

            def add(ph, i, n):
                stage, j = divmod(n, pairs(ph))
                a, b = 2 * j, 2 * j + 2
                ring = prod_ring(ph)
                k = n - pairs(ph)
                from_bank = ring[k % len(ring)][:, :].rearrange("p (t f) -> p t f", f=D)
                if (ph, stage) in (("edges1", 1), ("edges2", 1), ("nodes", 1)):
                    if ph != "nodes":
                        h = a // HALF
                        dve.wait_ge(resid_stored[h].sem, resid_stored[h].at(ph, i, -1))
                    dve.wait_ge(product.sem, product.at(ph, i, k))
                    v.tensor_tensor(resid[:, a:b, :], from_bank, rows[:, a:b, :],
                                    ALU.add).then_inc(resid_ready.sem, 1)
                if (ph, stage) == ("edges3", 0):
                    h = a // HALF
                    dve.wait_ge(resid_stored[h].sem, resid_stored[h].at(ph, i, -1))
                    v.tensor_tensor(resid[:, a:b, :], rows[:, a:b, :], got_e[:, a:b, :],
                                    ALU.add).then_inc(resid_ready.sem, 1)
                if (ph, stage) == ("nodes", 2):
                    dve.wait_ge(skip_ready.sem, skip_ready.at(ph, i, j))
                    dve.wait_ge(product.sem, product.at(ph, i, k))
                    v.tensor_tensor(resid3[:, a:b, :], from_bank, skip[:, a:b, :],
                                    ALU.add).then_inc(resid_ready.sem, 1)

            def measure(ph, i, n):
                stage, j = divmod(n, pairs(ph))
                if (ph, stage) in (("edges1", 1), ("edges2", 1), ("edges3", 0), ("nodes", 1)):
                    dve.wait_ge(resid_ready.sem, resid_ready.at(ph, i, j))
                if (ph, stage) == ("nodes", 2):
                    dve.wait_ge(resid_ready.sem, resid_ready.at(ph, i, NPAIR + j))
                if (ph, stage) in (("edges4", 1), ("nodes", 3)):
                    dve.wait_ge(product.sem, product.at(ph, i, n - pairs(ph)))
                for g, rows_ in source(ph, n):
                    last = v.bn_stats(stats[:, g, :], rows_)
                last.then_inc(stats_done.sem, 1)

            def aggregate(ph, i, n):
                dve.wait_ge(stats_done.sem, stats_done.at(ph, i, n))
                dve.sem_inc(dve_past, 1)
                for g, _ in source(ph, n):
                    last = v.bn_aggr(moments[:, g, :], stats[:, g, :])
                last.then_inc(moments_ready.sem, 1)

            def normalise(ph, i, n):
                dve.wait_ge(rstd_ready.sem, rstd_ready.at(ph, i, n))
                for g, rows_ in source(ph, n):
                    last = v.tensor_scalar(left[:, g, :], rows_, moments[:, g, 0:1],
                                           rstd[:, g:g + 1], ALU.subtract, ALU.mult)
                last.then_inc(normed.sem, 1)

            def relu_plus(ph, i, n, gathered_rows):
                stage, j = divmod(n, pairs(ph))
                a, b = 2 * j, 2 * j + 2
                dve.wait_ge(normed.sem, normed.at(ph, i, n))
                v.scalar_tensor_tensor(left[:, a:b, :], left[:, a:b, :], 0.0, gathered_rows[:, a:b, :],
                                       ALU.max, ALU.add).then_inc(plus_ready.sem, 1)

            def message_free(ph, i, j, back):
                dve.wait_ge(summed.sem, summed.at(ph, i, 2 * j + 1 - EG * (1 + back)))

            def relu_message(ph, i, n, record, back):
                message_free(ph, i, n % EP, back)
                dve.wait_ge(normed.sem, normed.at(ph, i, n))
                for g, _ in source(ph, n):
                    last = v.tensor_scalar(message(g), left[:, g, :], 0.0, record[:, g, COEF[ph]:COEF[ph] + 1],
                                           ALU.max, ALU.mult)
                last.then_inc(message_ready.sem, 1)

            def product_message(ph, i, j, record, back):
                ring = prod_ring(ph)
                k = EP + j
                message_free(ph, i, j, back)
                dve.wait_ge(product.sem, product.at(ph, i, k - back * steps(ph)))
                for t in range(2):
                    g = 2 * j + t
                    last = v.tensor_scalar(message(g), ring[k % len(ring)][:, t * D:t * D + D],
                                           record[:, g, COEF[ph]:COEF[ph] + 1], None, ALU.mult)
                last.then_inc(message_ready.sem, 1)

            def compare_sources(ph, i, j):
                dve.wait_ge(summed.sem, summed.at(ph, i, 2 * j + 1 - EG))
                dve.wait_ge(src_spread.sem, src_spread.at(ph, i, j // 2))
                at = 2 * j % 4 * P
                v.tensor_tensor(same[:, 2 * j:2 * j + 2, :],
                                spread_bank[:, at:at + 2 * P].rearrange("p (t f) -> p t f", f=P),
                                rec_now[:, 2 * j:2 * j + 2, R_SRC:R_SRC + 1].to_broadcast([P, 2, P]), ALU.is_equal)
                for t in range(2):
                    g = 2 * j + t
                    spread = spread_bank[:, g % 4 * P:g % 4 * P + P]
                    before = (rec_now if g else rec_before)[:, (g - 1) % EG, R_SRC:R_SRC + 1]
                    last = v.tensor_scalar(goes_on[:, g, :], spread, before, is_last[:, :],
                                           ALU.is_equal, ALU.mult)
                last.then_inc(same_ready.sem, 1)

            COEF = {"edges1": R_C1, "edges2": R_C2, "edges3": R_C3, "edges4": R_C3}

            def wait_gathered(ph, i, h):
                a, b = HALVES[h]
                dve.wait_ge(gathered[h].sem, gathered[h].at(ph, i, b - a - 1))

            def edges_slot(ph, i, n, main, before):
                old = rec_before if main else rec_now
                if n == 0 and main:
                    if before:
                        v.tensor_copy(rec_before[:, :, :].rearrange("p t f -> p (t f)"),
                                      rec_now[:, :, :].rearrange("p t f -> p (t f)")).then_inc(rec_kept.sem, 1)
                    else:
                        dve.wait_ge(message_ready.sem, message_ready.at(ph, i, -1))
                        v.memset(rec_before[:, :, :], -1.0).then_inc(rec_kept.sem, 1)
                    dve.wait_ge(rec_kept.sem, rec_kept.at(ph, i, 0))
                    dve.wait_ge(rec_loaded.sem, rec_loaded.at(ph, i, 0))
                    v.tensor_copy(rec_now[:, :, :].rearrange("p t f -> p (t f)"),
                                  rec_land[:, :]).then_inc(work_ready.sem, 1)
                if main and 2 * n in (0, HALF):
                    h = 2 * n // HALF
                    if ph in ("edges1", "edges3"):
                        wait_gathered(ph, i, h)
                    if ph != "edges1":
                        dve.wait_ge(rows_loaded[h].sem, rows_loaded[h].at(ph, i, 0))
                if main:
                    add(ph, i, n)
                    measure(ph, i, n)
                if n > 0 and main or n == 0 and before:
                    normalise(ph, i, n - 1)
                if main:
                    aggregate(ph, i, n)
                if ph in ("edges2", "edges4"):
                    if main and 1 <= n <= EP:
                        if 2 * (n - 1) in (0, HALF):
                            wait_gathered(ph, i, 2 * (n - 1) // HALF)
                        relu_plus(ph, i, n - 1, got_e)
                    if main and n >= EP + MESSAGE_AFTER:
                        product_message(ph, i, n - EP - MESSAGE_AFTER, rec_now, 0)
                    j = n + steps(ph) - EP - MESSAGE_AFTER
                    if before and j < EP:
                        product_message(ph, i, j, old, 1)
                elif main and n - 1 >= steps(ph) - EP:
                    relu_message(ph, i, n - 1, rec_now, 0)
                elif before and n == 0:
                    relu_message(ph, i, -1, old, 1)
                for j in range(EP):
                    if main and compare_slot(ph, j) == n:
                        compare_sources(ph, i, j)
                j = n - 5
                if ph == "edges2" and before and 0 <= j < EP:
                    h = 2 * j // HALF
                    dve.wait_ge(table_stored[h].sem, table_stored[h].at(ph, i - 1, -1))
                    dve.wait_ge(column_stored[h].sem, column_stored[h].at(ph, i - 1, -1))
                    for g in (2 * j, 2 * j + 1):
                        dve.wait_ge(sums_copied.sem, sums_copied.at(ph, i, g - EG))
                        last = v.tensor_tensor(pre[:, g, :], sums[:, g, :], b_sum[:, :], ALU.add)
                    last.then_inc(biased.sem, 1)
                j = n - 6
                if ph == "edges2" and before and 0 <= j < EP:
                    a, b = 2 * j, 2 * j + 2
                    dve.wait_ge(biased.sem, biased.at(ph, i, j - EP))
                    v.scalar_tensor_tensor(pre[:, a:b, :], pre[:, a:b, :], ALPHA, pre[:, a:b, :],
                                           ALU.mult, ALU.max).then_inc(leaky_ready.sem, 1)

            for ph, passes in PHASES[:-1]:
                for n in range(steps(ph)):
                    edges_slot(ph, 0, n, True, False)
                with dve.Fori(1, passes) as i:
                    for n in range(steps(ph)):
                        edges_slot(ph, i, n, True, True)
                for n in range(steps(ph)):
                    edges_slot(ph, passes, n, False, True)

            ph = "nodes"

            def nodes_slot(i, n, main, before):
                s, j = divmod(n, NPAIR)
                if main and n == 0:
                    dve.wait_ge(rec_loaded.sem, rec_loaded.at(ph, i, 0))
                    v.tensor_copy(node_now[:, :, :].rearrange("p t f -> p (t f)"),
                                  node_land[:, :]).then_inc(work_ready.sem, 1)
                if before and s == 0:
                    a, b, k = 2 * j, 2 * j + 2, 3 * NPAIR + j
                    ring = prod_ring(ph)
                    if j == 0:
                        dve.wait_ge(out_stored.sem, out_stored.at(ph, i, -2))
                    dve.wait_ge(product.sem, product.at(ph, i, k - SLOTS))
                    v.tensor_tensor(pre[:, a:b, :], ring[k % len(ring)][:, :].rearrange("p (t f) -> p t f", f=D),
                                    got[:, a:b, 3 * D:4 * D], ALU.add).then_inc(pre_ready.sem, 1)
                m = pair_at(n, 6)
                if before and m is not None:
                    a, b = 2 * m, 2 * m + 2
                    dve.wait_ge(silu_ready.sem, silu_ready.at(ph, i, m - NPAIR))
                    v.tensor_tensor(pre[:, a:b, :], resid3[:, a:b, :], pre[:, a:b, :],
                                    ALU.add).then_inc(out_ready.sem, 1)
                if main:
                    add(ph, i, n)
                m = pair_at(n, 1)
                if before and m is not None:
                    dve.wait_ge(pre_ready.sem, pre_ready.at(ph, i, m - NPAIR))
                    for g in (2 * m, 2 * m + 1):
                        last = v.bn_stats(stats_l[:, g, :], pre[:, g, :])
                    last.then_inc(stats_done_l.sem, 1)
                if main:
                    if n == 0:
                        dve.wait_ge(rows_loaded[0].sem, rows_loaded[0].at(ph, i, 0))
                    measure(ph, i, n)
                if n > 0 and main or n == 0 and before:
                    normalise(ph, i, n - 1)
                if main:
                    aggregate(ph, i, n)
                if before and m is not None:
                    dve.wait_ge(stats_done_l.sem, stats_done_l.at(ph, i, m - NPAIR))
                    dve.sem_inc(dve_past, 1)
                    for g in (2 * m, 2 * m + 1):
                        last = v.bn_aggr(moments_l[:, g, :], stats_l[:, g, :])
                    last.then_inc(moments_ready_l.sem, 1)
                if main and 1 <= n and (n - 1) // NPAIR in (1, 2):
                    if n - 1 == NPAIR:
                        dve.wait_ge(gathered[0].sem, gathered[0].at(ph, i, NG - 1))
                    relu_plus(ph, i, n - 1, got[:, :, 0:D] if (n - 1) // NPAIR == 1 else got[:, :, 2 * D:3 * D])
                m = pair_at(n, 2)
                if before and m is not None:
                    dve.wait_ge(moments_ready_l.sem, moments_ready_l.at(ph, i, m - NPAIR))
                    for g in (2 * m, 2 * m + 1):
                        last = v.scalar_tensor_tensor(pre[:, g, :], pre[:, g, :], moments_l[:, g, 0:1],
                                                      g_last[:, :], ALU.subtract, ALU.mult)
                    last.then_inc(gained.sem, 1)
                m = pair_at(n, 3)
                if before and m is not None:
                    dve.wait_ge(gained.sem, gained.at(ph, i, m - NPAIR))
                    dve.wait_ge(rstd_ready_l.sem, rstd_ready_l.at(ph, i, m - NPAIR))
                    for g in (2 * m, 2 * m + 1):
                        last = v.scalar_tensor_tensor(pre[:, g, :], pre[:, g, :], rstd_l[:, g:g + 1],
                                                      beta_last[:, :], ALU.mult, ALU.add)
                    last.then_inc(shifted.sem, 1)

            for n in range(SLOTS):
                nodes_slot(0, n, True, False)
            with dve.Fori(1, NGROUPS) as i:
                for n in range(SLOTS):
                    nodes_slot(i, n, True, True)
            for n in range(SLOTS):
                nodes_slot(NGROUPS, n, False, True)


_INS = ["x", "src", "dst", "edge_weight", "L1_gnn_W", "L1_gnn_b", "L1_gnn_W1", "L1_gnn_b1", "L1_gnn_W2", "L1_gnn_b2",
        "L2_gnn_W", "L2_gnn_b", "L3_gnn_W0", "L3_gnn_b0", "L3_gnn_g0", "L3_gnn_beta0", "L3_gnn_W1", "L3_gnn_b1",
        "L3_gnn_g1", "L3_gnn_beta1"]
_SCRATCH = {"node_tab": ((HI * LO, NF), F32), "rec_sorted": ((TILES * P, RF), F32),
            "state": ((EGROUPS, P, EG, D), F32),
            "table": ((TILES * P + 1, 4 * D), F32), "column0": ((TILES * P + 1, D), F32),
            "column1": ((TILES * P + 1, D), F32),
            "column2": ((TILES * P + 1, D), F32), "begin": ((5, D), F32)}


def kernel(**inputs):
    import numpy as _np
    import concourse.bacc as _bacc
    from concourse.bass_utils import run_bass_kernel_spmd as _run

    nc = _bacc.Bacc("TRN2", target_bir_lowering=False, num_devices=1)
    arrays, args = {}, {}
    for name in _INS:
        a = _np.ascontiguousarray(inputs[name])
        arrays[f"in_{name}"] = a
        args[name] = nc.dram_tensor(f"in_{name}", a.shape, mybir.dt.from_np(a.dtype), kind="ExternalInput").ap()
    out = nc.dram_tensor("out", (NODES, D), F32, kind="ExternalOutput").ap()
    scratch = {n: nc.dram_tensor(n, shape, dt).ap() for n, (shape, dt) in _SCRATCH.items()}
    gnn_stack(nc, args, out, scratch)
    r = _run(nc, [arrays], core_ids=[0])
    return r.results[0]["out"]
```
